# Optimizing a Trainium2 kernel written in Bass

```python
import numpy as np
import jax
import jax.numpy as jnp

def _softmax(x, axis=-1):
    return jax.nn.softmax(x, axis=axis)

def _gelu(x):
    return jax.nn.gelu(x, approximate=True)

def _silu(x):
    return jax.nn.silu(x)

def _sigmoid(x):
    return jax.nn.sigmoid(x)

def _layernorm(x, axis=-1, eps=1e-05):
    m = jnp.mean(x, axis=axis, keepdims=True)
    v = jnp.var(x, axis=axis, keepdims=True)
    return (x - m) / jnp.sqrt(v + eps)

def _scatter_add(tgt, idx, src, axis=0):
    return tgt.at[idx].add(src)

def _segment_sum(src, seg, n):
    return jax.ops.segment_sum(src, seg, n)
kernel_name = 'mk_cond_seq_d1_seqx_r2_8b4419'

def setup_inputs(seed: int=0):
    np.random.seed(seed)
    _w = jnp.asarray

    def _rec_inputs():
        import jax
        import jax.numpy as jnp
        _rk = jax.random.key(seed)
        x = -0.0003929 + 0.9999 * jax.random.normal(jax.random.fold_in(_rk, 1), (4, 1024, 512), jnp.float32)
        _lenS = 1024 - jax.random.randint(jax.random.fold_in(_rk, 7), (4,), 0, max(1, 1024 // 4) + 1, jnp.int32)
        _lenS2 = 1024 - jax.random.randint(jax.random.fold_in(_rk, 8), (4,), 0, max(1, 1024 // 4) + 1, jnp.int32)
        cond_256 = -0.0209273 + 1.04763 * jax.random.normal(jax.random.fold_in(_rk, 11), (4, 128), jnp.float32)
        return (x, cond_256)
    x, cond_256 = _rec_inputs()

    def _L0_cond_setup():
        import jax, jax.numpy as jnp
        import numpy as np
        EPS = 1e-06

        def act_quant(x):
            scale = 127.0 / jnp.clip(jnp.max(jnp.abs(x), axis=-1, keepdims=True), 1e-05, None)
            return jnp.clip(jnp.round(x * scale), -128.0, 127.0) / scale

        def weight_quant(w):
            scale = 1.0 / jnp.clip(jnp.mean(jnp.abs(w)), 1e-05, None)
            return jnp.clip(jnp.round(w * scale), -1.0, 1.0) / scale
        key = jax.random.key(seed)
        k0, k1, k2, k3, k4 = jax.random.split(key, 5)
        B, S, D, FF, C = (4, 2048, 512, 2048, 128)
        return {'x': jax.random.normal(k0, (B, S, D), jnp.float32), 'cond': jax.random.normal(k1, (B, C), jnp.float32), 'norm_w': jax.random.normal(k2, (D, C), jnp.float32) * 0.02, 'up_w': jax.random.normal(k3, (2 * FF, D), jnp.float32) * 0.02, 'down_w': jax.random.normal(k4, (D, FF), jnp.float32) * 0.02}
    _L0_cond_all = _L0_cond_setup()
    _L0_cond_in = {k: v for k, v in _L0_cond_all.items() if k in ('norm_w', 'up_w', 'down_w')}
    del _L0_cond_all
    return {'x': x, 'cond_256': cond_256, 'L0_cond_norm_w': _L0_cond_in['norm_w'], 'L0_cond_up_w': _L0_cond_in['up_w'], 'L0_cond_down_w': _L0_cond_in['down_w']}

def reference(x, cond_256, L0_cond_norm_w, L0_cond_up_w, L0_cond_down_w):
    import jax
    import jax.numpy as jnp

    def _L0_cond_ref(x, cond, norm_w, up_w, down_w):
        import jax, jax.numpy as jnp
        import numpy as np
        EPS = 1e-06

        def act_quant(x):
            scale = 127.0 / jnp.clip(jnp.max(jnp.abs(x), axis=-1, keepdims=True), 1e-05, None)
            return jnp.clip(jnp.round(x * scale), -128.0, 127.0) / scale

        def weight_quant(w):
            scale = 1.0 / jnp.clip(jnp.mean(jnp.abs(w)), 1e-05, None)
            return jnp.clip(jnp.round(w * scale), -1.0, 1.0) / scale
        scale = cond @ norm_w.T + 1.0
        ms = jnp.mean(x * x, axis=-1, keepdims=True)
        h = x * (scale[:, None, :] * jax.lax.rsqrt(ms + EPS))
        u = h @ up_w.T
        val, gate = jnp.split(u, 2, axis=-1)
        h = val * jax.nn.gelu(gate, approximate=False)
        hq = h + jax.lax.stop_gradient(act_quant(h) - h)
        wq = down_w + jax.lax.stop_gradient(weight_quant(down_w) - down_w)
        y = hq @ wq.T
        return y + x
    x = _L0_cond_ref(x, cond_256, L0_cond_norm_w, L0_cond_up_w, L0_cond_down_w)
    return x

_drawn_inputs = setup_inputs


def setup_inputs(seed=0):
    import zlib

    import numpy as np

    out = dict(_drawn_inputs(seed))
    spreads = {}
    factors = {}
    for name, (base, spread) in spreads.items():
        noise = np.random.default_rng([zlib.crc32(name.encode()), seed]).standard_normal(out[name].shape)
        drawn = base * np.exp(spread * noise) if base else spread * noise
        out[name] = jnp.asarray(drawn.astype(out[name].dtype))
    for name, factor in factors.items():
        out[name] = (out[name] * factor).astype(out[name].dtype)
    return out
```

```python
from contextlib import ExitStack

import concourse.bass as bass
from concourse import mybir

P = 128
ALU = mybir.AluOpType
ACT = mybir.ActivationFunctionType
F32 = mybir.dt.float32
I32 = mybir.dt.int32
FP16 = mybir.dt.float16
BF16 = mybir.dt.bfloat16
AX = mybir.AxisListType
RADD = bass.bass_isa.ReduceOp.add
RMAX = bass.bass_isa.ReduceOp.max

ROUND = 1.5 * 2.0 ** 23
EXPONENT = 0x7F800000
RSQRT_SEED = 0x5F3759DF
W_TOP = 2.0 ** 14
X_TOP = 2.0 ** 10
EPS = 1e-6
QMAX = 127.0
CLIP = 1e-5


def bass_cond_norm_geglu_bitlinear(
    nc: bass.Bass,
    x_rows: bass.AP,
    x_cols: bass.AP,
    cond_t: bass.AP,
    norm_t: bass.AP,
    up_t: bass.AP,
    down_t: bass.AP,
    out: bass.AP,
):
    T, D = x_rows.shape
    NB, _, cols = x_cols.shape
    C, B = cond_t.shape
    J = up_t.shape[0]
    KT = D // P
    TB = T // NB
    TT = TB // P
    WJ = 2 * KT * P
    PER_B = NB // B
    DC = WJ // D
    ND = J // DC
    XS = 3
    assert C == P and TB == 512 and D == 512 and cols == KT * TB and J == 16 and WJ == DC * D

    x_rows = x_rows.rearrange("(b p i) d -> b p (i d)", p=P, i=TT)
    out = out.rearrange("(b p i) d -> b p (i d)", p=P, i=TT)

    ds = bass.ds

    with ExitStack() as ctx:
        def sb(name, shape, dt):
            return ctx.enter_context(nc.sbuf_tensor(name, shape, dt))

        def sem(name):
            return ctx.enter_context(nc.semaphore(name))

        w_hi = sb("w_hi", [P, J * WJ], FP16)
        w_lo = sb("w_lo", [P, J * WJ], FP16)
        w_unscale = sb("w_unscale", [P, J], F32)
        dw = sb("dw", [P, J * D], BF16)
        up_raw = sb("up_raw", [P, 2, WJ], F32)
        down_raw = sb("down_raw", [P, 2, WJ], F32)
        xt_raw = sb("xt_raw", [P, KT * TB], F32)
        xr = sb("xr", [P, XS * TT * D], F32)
        xn = sb("xn", [P, 2, TB], F32)
        x_hi = sb("x_hi", [P, 2 * KT * TB], FP16)
        x_lo = sb("x_lo", [P, 2 * KT * TB], FP16)
        g = sb("g", [P, 2, TB], F32)
        h = sb("h", [P, J * TB], F32)
        h_max = sb("h_max", [P, TB], F32)
        scaled = sb("scaled", [P, 2, TB], F32)
        q = sb("q", [P, J * TB], BF16)
        sum_junk = q[:, 0:2 * WJ]
        square_junk = [q[:, 2 * WJ + k * TT * D:2 * WJ + (k + 1) * TT * D] for k in range(2)]
        square_junk.append(up_raw[:, 0, :].bitcast(BF16))
        cond_sb = sb("cond_sb", [P, B], F32)
        norm_sb = scaled[:, 0, :]
        cs_raw = sb("cs_raw", [P, KT * B], F32)
        cs = sb("cs", [P, KT * B], F32)
        cs_unscale = sb("cs_unscale", [P, 1], F32)
        peak = sb("peak", [P, 2], F32)
        peak_all = sb("peak_all", [P, 2], F32)
        p2 = sb("p2", [P, 2], F32)
        p2_inv = sb("p2_inv", [P, 2], F32)
        w_scale = sb("w_scale", [P, 2], F32)
        sumsq = sb("sumsq", [P, TT], F32)
        ms = sb("ms", [P, TT], F32)
        rs = sb("rs", [P, TT], F32)
        rs_t = sb("rs_t", [P, TT], F32)
        row_max = sb("row_max", [P, TT], F32)
        row_rec = sb("row_rec", [P, TT], F32)
        row_scale = sb("row_scale", [P, TT], F32)
        dequant = sb("dequant", [P, TT], F32)
        d_sums = sb("d_sums", [P, ND], F32)
        d_sum = sb("d_sum", [P, 1], F32)
        d_total = sb("d_total", [P, 1], F32)
        d_mean = sb("d_mean", [P, 1], F32)
        d_scale = sb("d_scale", [P, 1], F32)
        ident = sb("ident", [P, P], F32)

        ps_u = ctx.enter_context(nc.psum_tensor("ps_u", [P, 4, 512], F32))
        ps_y = ctx.enter_context(nc.psum_tensor("ps_y", [P, 2, 512], F32))
        ps_m = ctx.enter_context(nc.psum_tensor("ps_m", [P, 512], F32))
        ps_s = ctx.enter_context(nc.psum_tensor("ps_s", [P, 512], F32))

        consts_loaded = sem("consts_loaded")
        ident_ready = sem("ident_ready")
        up_loaded = [sem("up_loaded0"), sem("up_loaded1")]
        down_loaded = [sem("down_loaded0"), sem("down_loaded1")]
        xt_loaded = sem("xt_loaded")
        xr_loaded = sem("xr_loaded")
        y_stored = sem("y_stored")
        cs_matmul = sem("cs_matmul")
        cs_step = sem("cs_step")
        cs_peak = sem("cs_peak")
        cs_peak_all = sem("cs_peak_all")
        w_peak = sem("w_peak")
        w_peak_all = sem("w_peak_all")
        w_step = sem("w_step")
        w_scaled = sem("w_scaled")
        w_hi_ready = sem("w_hi_ready")
        w_ready = sem("w_ready")
        d_summed = sem("d_summed")
        d_sum_ready = sem("d_sum_ready")
        d_total_ready = sem("d_total_ready")
        d_step = sem("d_step")
        d_scale_ready = sem("d_scale_ready")
        d_pass = sem("d_pass")
        dw_ready = sem("dw_ready")
        sumsq_ready = sem("sumsq_ready")
        rs_step = sem("rs_step")
        rs_ready = sem("rs_ready")
        rs_rows = sem("rs_rows")
        xn_ready = sem("xn_ready")
        x_hi_ready = sem("x_hi_ready")
        x_lo_ready = sem("x_lo_ready")
        val_ready = sem("val_ready")
        gate_ready = sem("gate_ready")
        g_ready = sem("g_ready")
        h_abs_ready = sem("h_abs_ready")
        h_ready = sem("h_ready")
        h_max_ready = sem("h_max_ready")
        max_rows = sem("max_rows")
        row_step = sem("row_step")
        scale_ready = sem("scale_ready")
        dequant_ready = sem("dequant_ready")
        scale_rows = sem("scale_rows")
        scaled_ready = sem("scaled_ready")
        q_ready = sem("q_ready")
        y_ready = sem("y_ready")
        y_done = sem("y_done")

        RS_STEPS = 14

        block = ctx.enter_context(nc.Block())

        @block.sync
        def _(sp):
            def load_up(j, slot):
                sp.dma_start(up_raw[:, slot, :], up_t[j]).then_inc(up_loaded[slot], 16)

            def load_down(chunk, slot):
                sp.dma_start(down_raw[:, slot, :], down_t[:, ds(chunk * WJ, WJ)]).then_inc(down_loaded[slot], 16)

            def load_x(b):
                if not isinstance(b, int) or b >= 1:
                    sp.wait_ge(xn_ready, b * KT)
                sp.dma_start(xt_raw[:], x_cols[b]).then_inc(xt_loaded, 16)
                if not isinstance(b, int) or b >= XS:
                    sp.wait_ge(y_stored, (b - XS + 1) * TT * 16)
                sp.dma_start(xr[:, ds((b % XS) * (TT * D), TT * D)], x_rows[b]).then_inc(xr_loaded, 16)

            def store_y(b):
                for i in range(TT):
                    sp.wait_ge(y_done, b * TT + i + 1)
                    sp.dma_start(out[b][:, i * D:(i + 1) * D], xr[:, ds((b % XS) * (TT * D) + i * D, D)]).then_inc(y_stored, 16)

            sp.dma_start(cond_sb[:], cond_t).then_inc(consts_loaded, 16)
            sp.dma_start(norm_sb, norm_t).then_inc(consts_loaded, 16)
            load_up(0, 0)
            load_x(0)
            load_up(1, 1)
            load_x(1)
            load_down(0, 0)
            load_down(1, 1)
            def next_up(i, slot):
                sp.wait_ge(w_ready, 2 * i + slot - 1)
                load_up(2 * i + slot, slot)

            def next_down(i, slot):
                sp.wait_ge(d_summed, 2 * i + slot - 1)
                load_down((2 * i + slot) % ND, slot)

            with sp.Fori(1, ND // 2) as i:
                for s in range(2):
                    next_up(i, s)
                    next_down(i, s)
            with sp.Fori(ND // 2, J // 2) as i:
                for s in range(2):
                    next_up(i, s)
            load_x(2)
            with sp.Fori(ND // 2, ND) as i:
                for s in range(2):
                    next_down(i, s)
            store_y(0)
            with sp.Fori(XS, NB) as b:
                load_x(b)
                store_y(b - 2)
            store_y(NB - 2)
            store_y(NB - 1)
            sp.wait_ge(y_stored, NB * TT * 16)

        @block.tensor
        def _(pe):
            def up_half(b, j, s, which):
                bank = ps_u[:, 2 * s + which, :]
                done = (val_ready, gate_ready)[which]
                for kt in range(KT):
                    w_at = ds(j * WJ + (which * KT + kt) * P, P)
                    x_at = ds((b % 2) * (KT * TB) + kt * TB, TB)
                    pe.matmul(bank, w_hi[:, w_at], x_hi[:, x_at], start=(kt == 0), stop=False)
                    pe.matmul(bank, w_hi[:, w_at], x_lo[:, x_at], start=False, stop=False)
                    last = pe.matmul(bank, w_lo[:, w_at], x_hi[:, x_at], start=False, stop=(kt == KT - 1))
                last.then_inc(done, 1)

            def gate(b, j, s, first=False, prep=False):
                n = b * J + j
                if prep:
                    pe.wait_ge(w_ready, j + 1)
                if not first:
                    pe.wait_ge(g_ready, n - 1)
                up_half(b, j, s, 1)

            def val(b, j, s, first=False):
                n = b * J + j
                if not first:
                    pe.wait_ge(h_ready, n - 1)
                up_half(b, j, s, 0)

            def turn_max(b):
                pe.wait_ge(h_max_ready, (b + 1) * J)
                if not isinstance(b, int) or b < NB - 1:
                    pe.wait_ge(xn_ready, (b + 2) * KT)
                else:
                    pe.wait_ge(xn_ready, NB * KT)
                for i in range(TT):
                    last = pe.transpose(ps_m[:, i * P:(i + 1) * P], h_max[:, i * P:(i + 1) * P], ident[:])
                last.then_inc(max_rows, 1)

            def spread_scale(b):
                pe.wait_ge(scale_ready, b + 1)
                for i in range(TT):
                    last = pe.transpose(ps_s[:, i * P:(i + 1) * P], row_scale[:, i:i + 1].to_broadcast([P, P]), ident[:])
                last.then_inc(scale_rows, 1)

            def spread_rs(b):
                pe.wait_ge(rs_ready, b + 1)
                if not isinstance(b, int) or b >= 2:
                    pe.wait_ge(scale_ready, b - 1)
                for i in range(TT):
                    last = pe.transpose(ps_m[:, i * P:(i + 1) * P], rs[:, i:i + 1].to_broadcast([P, P]), ident[:])
                last.then_inc(rs_rows, 1)

            def down(b, i):
                if i >= 2:
                    pe.wait_ge(y_done, b * TT + i - 1)
                for j in range(J):
                    last = pe.matmul(ps_y[:, i % 2, :], q[:, j * TB + i * P:j * TB + (i + 1) * P],
                                     dw[:, j * D:(j + 1) * D], start=(j == 0), stop=(j == J - 1))
                last.then_inc(y_ready, 1)

            def up_block(b, first=False, last=False):
                pe.wait_ge(x_lo_ready, (b + 1) * KT)
                pe.wait_ge(x_hi_ready, (b + 1) * KT)
                gate(b, 0, 0, first, first)
                if not first:
                    turn_max(b - 1)
                val(b, 0, 0, first)
                if not first:
                    spread_scale(b - 1)
                gate(b, 1, 1, first, first)
                val(b, 1, 1, first)
                with pe.Fori(1, 4) as i:
                    for s in range(2):
                        gate(b, 2 * i + s, s, prep=first)
                        val(b, 2 * i + s, s)
                if not last:
                    spread_rs(b + 1)
                if not first:
                    pe.wait_ge(q_ready, b * J)
                    pe.wait_ge(dw_ready, ND)
                for i in range(4):
                    gate(b, 8 + i, i % 2, prep=first)
                    val(b, 8 + i, i % 2)
                    if not first:
                        down(b - 1, i)
                with pe.Fori(6, 8) as i:
                    for s in range(2):
                        gate(b, 2 * i + s, s, prep=first)
                        val(b, 2 * i + s, s)

            pe.wait_ge(consts_loaded, 32)
            for kt in range(KT):
                last = pe.matmul(ps_y[:, 0, kt * B:(kt + 1) * B], norm_sb[:, kt * P:(kt + 1) * P], cond_sb[:],
                                 start=True, stop=True)
            last.then_inc(cs_matmul, 1)
            pe.wait_ge(ident_ready, 1)
            spread_rs(0)
            up_block(0, first=True)
            with pe.Fori(1, NB - 1) as b:
                up_block(b)
            up_block(NB - 1, last=True)
            turn_max(NB - 1)
            spread_scale(NB - 1)
            pe.wait_ge(h_ready, NB * J)
            for j in range(J):
                pe.wait_ge(q_ready, (NB - 1) * J + j + 1)
                for i in range(TT):
                    last = pe.matmul(ps_u[:, i, :], q[:, j * TB + i * P:j * TB + (i + 1) * P],
                                     dw[:, j * D:(j + 1) * D], start=(j == 0), stop=(j == J - 1))
                    if j == J - 1:
                        last.then_inc(y_ready, 1)

        @block.scalar
        def _(act):
            def gelu(b, j, s, first=False):
                n = b * J + j
                act.wait_ge(gate_ready, n + 1)
                if first:
                    act.wait_ge(w_scaled, 2)
                else:
                    act.wait_ge(h_max_ready, n - 1)
                act.activation(g[:, s, :], ps_u[:, 2 * s + 1, :], ACT.Gelu,
                               scale=w_unscale[:, ds(j, 1)]).then_inc(g_ready, 1)

            def absolute(b, j, s):
                act.wait_ge(h_ready, b * J + j + 1)
                act.activation(g[:, s, :], h[:, ds(j * TB, TB)], ACT.Abs).then_inc(h_abs_ready, 1)

            def squares(b):
                act.wait_ge(xr_loaded, (b + 1) * 16)
                if not isinstance(b, int) or b >= 1:
                    act.wait_ge(rs_ready, b)
                junk = square_junk[b if isinstance(b, int) and b <= 1 else 2]
                for i in range(TT):
                    last = act.activation(junk[:, i * D:(i + 1) * D], xr[:, ds((b % XS) * (TT * D) + i * D, D)], ACT.Square,
                                          accum_out=sumsq[:, i:i + 1])
                last.then_inc(sumsq_ready, 1)

            def high(b, kt):
                act.wait_ge(xn_ready, b * KT + kt + 1)
                if not isinstance(b, int) or b >= 2:
                    act.wait_ge(val_ready, (b - 1) * J)
                act.copy(x_hi[:, ds((b % 2) * (KT * TB) + kt * TB, TB)], xn[:, kt % 2, :]).then_inc(x_hi_ready, 1)

            def weight_high(j, slot):
                act.wait_ge(w_scaled, j + 1)
                act.activation(w_hi[:, ds(j * WJ, WJ)], up_raw[:, slot, :], ACT.Copy,
                               scale=w_scale[:, slot:slot + 1]).then_inc(w_hi_ready, 1)

            def sum_down(chunk, slot):
                act.wait_ge(down_loaded[slot], ((chunk - slot) // 2 + 1) * 16)
                if not isinstance(chunk, int) or chunk >= 2:
                    act.wait_ge(d_summed, chunk - 1)
                act.activation(sum_junk[:, slot * WJ:(slot + 1) * WJ], down_raw[:, slot, :], ACT.Abs,
                               accum_out=d_sums[:, ds(chunk, 1)]).then_inc(d_summed, 1)

            squares(0)
            weight_high(0, 0)
            for kt in range(KT):
                high(0, kt)
            weight_high(1, 1)
            def first_pair(j, s, peeled=False):
                gelu(0, j, s, first=peeled)
                absolute(0, j, s)
                weight_high(j + 2, s)

            for s in range(2):
                first_pair(s, s, peeled=True)
                sum_down(s, s)
            with act.Fori(1, 4) as i:
                for s in range(2):
                    first_pair(2 * i + s, s)
                    sum_down(2 * i + s, s)
            squares(1)
            for k in range(4):
                first_pair(8 + k, k % 2)
                high(1, k)
            for s in range(2):
                first_pair(J - 4 + s, s)
            for s in range(2):
                gelu(0, J - 2 + s, s)
                absolute(0, J - 2 + s, s)

            def pair(b, j, s):
                gelu(b, j, s)
                absolute(b, j, s)

            def up_block(b, last=False):
                with act.Fori(0, 4) as i:
                    for s in range(2):
                        pair(b, 2 * i + s, s)
                if not last:
                    squares(b + 1)
                for k in range(4):
                    pair(b, 8 + k, k % 2)
                    if not last:
                        high(b + 1, k)
                with act.Fori(6, 8) as i:
                    for s in range(2):
                        pair(b, 2 * i + s, s)

            with act.Fori(1, NB - 1) as b:
                up_block(b)
            up_block(NB - 1, last=True)

        @block.gpsimd
        def _(pool):
            pool.memset(ident[:], 0.0).then_inc(ident_ready, 1)
            pool.wait_ge(ident_ready, 1)
            pool.affine_select(out=ident[:], in_=ident[:], compare_op=ALU.not_equal, fill=1.0, base=0,
                               pattern=[[-1, P]], channel_multiplier=1).then_inc(ident_ready, 1)
            pool.wait_ge(cs_peak, 1)
            pool.partition_all_reduce(peak_all[:, 0:1], peak[:, 0:1], P, RMAX).then_inc(cs_peak_all, 1)
            for j in range(J):
                s = j % 2
                pool.wait_ge(w_peak, j + 1)
                pool.partition_all_reduce(peak_all[:, s:s + 1], peak[:, s:s + 1], P, RMAX).then_inc(w_peak_all, 1)
                if j == 9:
                    pool.wait_ge(d_sum_ready, 1)
                    pool.partition_all_reduce(d_total[:], d_sum[:], P, RADD).then_inc(d_total_ready, 1)
            pool.wait_ge(d_scale_ready, 1)
            for i in range(ND // 2):
                for s in range(2):
                    c = 2 * i + s
                    raw = down_raw[:, s, :]
                    pool.wait_ge(down_loaded[s], (ND // 2 + i + 1) * 16)
                    pool.tensor_scalar(raw, raw, d_scale[:], ROUND, ALU.mult, ALU.add).then_inc(d_pass, 1)
                    pool.wait_ge(d_pass, 2 * c + 1)
                    pool.tensor_scalar(raw, raw, -ROUND, 1.0, ALU.add, ALU.mult).then_inc(d_pass, 1)
                    pool.wait_ge(d_pass, 2 * c + 2)
                    pool.tensor_scalar(dw[:, ds(c * WJ, WJ)], raw, 1.0, -1.0, ALU.min, ALU.max).then_inc(dw_ready, 1)
                    pool.wait_ge(dw_ready, c + 1)
                    pool.sem_inc(d_summed, 1)

        @block.vector
        def _(dve):
            def weight_peak(j, slot):
                dve.wait_ge(up_loaded[slot], ((j - slot) // 2 + 1) * 16)
                if not isinstance(j, int) or j >= 2:
                    dve.wait_ge(w_peak_all, j - 1)
                dve.tensor_reduce(peak[:, slot:slot + 1], up_raw[:, slot, :], AX.X, ALU.max,
                                  apply_absolute_value=True).then_inc(w_peak, 1)

            def power_of_two(slot, step, count):
                a, p, pi = peak_all[:, slot:slot + 1], p2[:, slot:slot + 1], p2_inv[:, slot:slot + 1]
                dve.tensor_scalar(a, a, 2.0 ** -100, 2.0 ** 110, ALU.max, ALU.min).then_inc(step, 1)
                dve.wait_ge(step, count + 1)
                dve.tensor_scalar(p.bitcast(I32), a.bitcast(I32), EXPONENT, None, ALU.bitwise_and).then_inc(step, 1)
                dve.wait_ge(step, count + 2)
                dve.reciprocal(pi, p).then_inc(step, 1)
                dve.wait_ge(step, count + 3)

            def weight_scale(j, slot):
                dve.wait_ge(w_peak_all, j + 1)
                power_of_two(slot, w_step, 4 * j)
                dve.tensor_scalar(w_unscale[:, ds(j, 1)], p2[:, slot:slot + 1], cs_unscale[:], None,
                                  ALU.mult).then_inc(w_step, 1)
                dve.wait_ge(w_step, 4 * j + 4)
                dve.tensor_scalar(w_scale[:, slot:slot + 1], p2_inv[:, slot:slot + 1], W_TOP, None,
                                  ALU.mult).then_inc(w_scaled, 1)

            def weight_low(j, slot):
                dve.wait_ge(w_scaled, j + 1)
                dve.wait_ge(w_hi_ready, j + 1)
                at = ds(j * WJ, WJ)
                dve.scalar_tensor_tensor(out=w_lo[:, at], in0=up_raw[:, slot, :], scalar=w_scale[:, slot:slot + 1],
                                         in1=w_hi[:, at], op0=ALU.mult, op1=ALU.subtract).then_inc(w_ready, 1)

            def rsqrt(b):
                base = b * RS_STEPS
                dve.wait_ge(sumsq_ready, b + 1)
                if not isinstance(b, int) or b >= 1:
                    dve.wait_ge(rs_rows, b)
                dve.tensor_scalar(ms[:], sumsq[:], 1.0 / D, EPS, ALU.mult, ALU.add).then_inc(rs_step, 1)
                dve.wait_ge(rs_step, base + 1)
                dve.tensor_scalar(rs_t[:].bitcast(I32), ms[:].bitcast(I32), 1, None,
                                  ALU.logical_shift_right).then_inc(rs_step, 1)
                dve.wait_ge(rs_step, base + 2)
                dve.tensor_scalar(rs[:].bitcast(I32), rs_t[:].bitcast(I32), -1.0, float(RSQRT_SEED),
                                  ALU.mult, ALU.add).then_inc(rs_step, 1)
                dve.wait_ge(rs_step, base + 3)
                for k in range(3):
                    dve.tensor_tensor(rs_t[:], rs[:], rs[:], ALU.mult).then_inc(rs_step, 1)
                    dve.wait_ge(rs_step, base + 4 * k + 4)
                    dve.tensor_tensor(rs_t[:], rs_t[:], ms[:], ALU.mult).then_inc(rs_step, 1)
                    dve.wait_ge(rs_step, base + 4 * k + 5)
                    dve.tensor_scalar(rs_t[:], rs_t[:], -0.5, 1.5, ALU.mult, ALU.add).then_inc(rs_step, 1)
                    dve.wait_ge(rs_step, base + 4 * k + 6)
                    last = dve.tensor_tensor(rs[:], rs[:], rs_t[:], ALU.mult)
                    if k < 2:
                        last.then_inc(rs_step, 1)
                        dve.wait_ge(rs_step, base + 4 * k + 7)
                    else:
                        last.then_inc(rs_ready, 1)

            def norm(b, kt):
                dve.wait_ge(rs_rows, b + 1)
                dve.wait_ge(xt_loaded, (b + 1) * 16)
                if kt >= 2:
                    dve.wait_ge(x_lo_ready, b * KT + kt - 1)
                elif not isinstance(b, int) or b >= 1:
                    dve.wait_ge(x_lo_ready, b * KT + kt - 1)
                dve.scalar_tensor_tensor(out=xn[:, kt % 2, :], in0=xt_raw[:, kt * TB:(kt + 1) * TB],
                                         scalar=cs[:, ds(kt * B + b // PER_B, 1)], in1=ps_m[:],
                                         op0=ALU.mult, op1=ALU.mult).then_inc(xn_ready, 1)

            def low(b, kt):
                at = ds((b % 2) * (KT * TB) + kt * TB, TB)
                dve.wait_ge(x_hi_ready, b * KT + kt + 1)
                dve.tensor_tensor(x_lo[:, at], xn[:, kt % 2, :], x_hi[:, at], ALU.subtract).then_inc(x_lo_ready, 1)

            def hidden(b, j, s, first=False):
                n = b * J + j
                at = ds(j * TB, TB)
                dve.wait_ge(val_ready, n + 1)
                dve.wait_ge(g_ready, n + 1)
                if not first:
                    dve.wait_ge(scaled_ready, n - J + 1)
                dve.scalar_tensor_tensor(out=h[:, at], in0=ps_u[:, 2 * s, :], scalar=w_unscale[:, ds(j, 1)],
                                         in1=g[:, s, :], op0=ALU.mult, op1=ALU.mult).then_inc(h_ready, 1)

            def peak_of(b, j, s, first=False):
                n = b * J + j
                dve.wait_ge(h_abs_ready, n + 1)
                if isinstance(j, int) and j == 0:
                    if not first:
                        dve.wait_ge(max_rows, b)
                    dve.tensor_copy(h_max[:], g[:, s, :]).then_inc(h_max_ready, 1)
                else:
                    dve.wait_ge(h_max_ready, n)
                    dve.tensor_tensor(h_max[:], g[:, s, :], h_max[:], ALU.max).then_inc(h_max_ready, 1)

            def row_scales(b):
                dve.wait_ge(max_rows, b + 1)
                dve.tensor_reduce(row_max[:], ps_m[:].rearrange("p (i n) -> p i n", i=TT), AX.X,
                                  ALU.max).then_inc(row_step, 1)
                dve.wait_ge(row_step, 3 * b + 1)
                dve.tensor_scalar(row_max[:], row_max[:], CLIP, None, ALU.max).then_inc(row_step, 1)
                dve.wait_ge(row_step, 3 * b + 2)
                dve.reciprocal(row_rec[:], row_max[:]).then_inc(row_step, 1)
                dve.wait_ge(row_step, 3 * b + 3)
                dve.tensor_scalar(row_scale[:], row_rec[:], QMAX, None, ALU.mult).then_inc(scale_ready, 1)
                dve.tensor_scalar(dequant[:], row_max[:], 1.0 / QMAX, d_mean[:], ALU.mult,
                                  ALU.mult).then_inc(dequant_ready, 1)

            def quantize(b, t):
                for s in range(2):
                    m = b * J + t + s
                    if isinstance(t, int) and t == 0:
                        dve.wait_ge(scale_rows, b + 1)
                    if not (isinstance(t, int) and t == 0):
                        dve.wait_ge(q_ready, m - 1)
                    dve.tensor_tensor(scaled[:, s, :], h[:, ds((t + s) * TB, TB)], ps_s[:],
                                      ALU.mult).then_inc(scaled_ready, 1)
                for s in range(2):
                    m = b * J + t + s
                    dve.wait_ge(scaled_ready, m + 1)
                    dve.tensor_scalar(q[:, ds((t + s) * TB, TB)], scaled[:, s, :], ROUND, ROUND, ALU.add,
                                      ALU.subtract).then_inc(q_ready, 1)

            def residual(b, i, bank):
                at = ds((b % XS) * (TT * D) + i * D, D)
                dve.wait_ge(y_ready, b * TT + i + 1)
                dve.wait_ge(dequant_ready, b + 1)
                dve.scalar_tensor_tensor(out=xr[:, at], in0=bank, scalar=dequant[:, i:i + 1], in1=xr[:, at],
                                         op0=ALU.mult, op1=ALU.add).then_inc(y_done, 1)

            dve.wait_ge(cs_matmul, 1)
            dve.tensor_scalar(cs_raw[:], ps_y[:, 0, 0:KT * B], 1.0, None, ALU.add).then_inc(cs_step, 1)
            dve.wait_ge(cs_step, 1)
            dve.tensor_reduce(peak[:, 0:1], cs_raw[:], AX.X, ALU.max, apply_absolute_value=True).then_inc(cs_peak, 1)
            dve.wait_ge(cs_peak_all, 1)
            power_of_two(0, cs_step, 1)
            dve.tensor_scalar(cs_unscale[:], p2[:, 0:1], 1.0 / (W_TOP * X_TOP), None, ALU.mult).then_inc(cs_step, 1)
            dve.tensor_scalar(cs[:], cs_raw[:], p2_inv[:, 0:1], X_TOP, ALU.mult, ALU.mult).then_inc(cs_step, 1)
            dve.wait_ge(cs_step, 6)
            weight_peak(0, 0)
            rsqrt(0)
            weight_scale(0, 0)
            norm(0, 0)
            norm(0, 1)
            weight_low(0, 0)
            low(0, 0)
            low(0, 1)
            norm(0, 2)
            norm(0, 3)
            low(0, 2)
            low(0, 3)
            weight_peak(1, 1)
            weight_scale(1, 1)
            weight_low(1, 1)

            def hidden_first(j, s):
                weight_peak(j + 2, s)
                hidden(0, j, s, first=True)
                weight_scale(j + 2, s)
                weight_low(j + 2, s)
                peak_of(0, j, s, first=True)

            hidden_first(0, 0)
            hidden_first(1, 1)
            with dve.Fori(1, 4) as i:
                for s in range(2):
                    hidden_first(2 * i + s, s)
            dve.wait_ge(d_summed, ND)
            dve.tensor_reduce(d_sum[:], d_sums[:], AX.X, ALU.add).then_inc(d_sum_ready, 1)
            rsqrt(1)
            for k in range(4):
                hidden_first(8 + k, k % 2)
                norm(1, k)
                low(1, k)
            dve.wait_ge(d_total_ready, 1)
            dve.tensor_scalar(d_mean[:], d_total[:], 1.0 / (J * P * D), CLIP, ALU.mult, ALU.max).then_inc(d_step, 1)
            dve.wait_ge(d_step, 1)
            dve.reciprocal(d_scale[:], d_mean[:]).then_inc(d_scale_ready, 1)
            for s in range(2):
                hidden_first(J - 4 + s, s)
            for s in range(2):
                hidden(0, J - 2 + s, s, first=True)
                peak_of(0, J - 2 + s, s, first=True)

            def up_block(b, last=False):
                row_scales(b - 1)
                quantize(b - 1, 0)
                hidden(b, 0, 0)
                quantize(b - 1, 2)
                peak_of(b, 0, 0)
                hidden(b, 1, 1)
                quantize(b - 1, 4)
                peak_of(b, 1, 1)
                with dve.Fori(1, 3) as i:
                    for s in range(2):
                        hidden(b, 2 * i + s, s)
                        quantize(b - 1, 4 * i + 2 * s + 2)
                        peak_of(b, 2 * i + s, s)
                hidden(b, 6, 0)
                quantize(b - 1, J - 2)
                peak_of(b, 6, 0)
                hidden(b, 7, 1)
                peak_of(b, 7, 1)
                if not last:
                    rsqrt(b + 1)
                for k in range(4):
                    hidden(b, 8 + k, k % 2)
                    if not last:
                        norm(b + 1, k)
                        low(b + 1, k)
                    peak_of(b, 8 + k, k % 2)
                    residual(b - 1, k, ps_y[:, k % 2, :])
                with dve.Fori(6, 8) as i:
                    for s in range(2):
                        hidden(b, 2 * i + s, s)
                        peak_of(b, 2 * i + s, s)

            with dve.Fori(1, NB - 1) as b:
                up_block(b)
            up_block(NB - 1, last=True)
            row_scales(NB - 1)
            for t in range(0, J, 2):
                quantize(NB - 1, t)
            for i in range(TT):
                residual(NB - 1, i, ps_u[:, i, :])


def kernel(x, cond_256, L0_cond_norm_w, L0_cond_up_w, L0_cond_down_w):
    import numpy as _np
    import concourse.bacc as _bacc
    from concourse import mybir as _mybir
    from concourse.bass_utils import run_bass_kernel_spmd as _run

    x = _np.asarray(x)
    up, down = _np.asarray(L0_cond_up_w), _np.asarray(L0_cond_down_w)
    S0, S1, D = x.shape
    FF = down.shape[1]
    TB, KT, J = 512, D // 128, FF // 128
    rows = x.reshape(S0 * S1, D)
    laid = {
        "x_rows": rows,
        "x_cols": rows.reshape(-1, 128, TB // 128, KT, 128).transpose(0, 4, 3, 2, 1).reshape(-1, 128, KT * TB),
        "cond_t": _np.asarray(cond_256).T,
        "norm_t": _np.asarray(L0_cond_norm_w).T,
        "up_t": up.reshape(2, J, 128, KT, 128).transpose(1, 4, 0, 3, 2).reshape(J, 128, 2 * KT * 128),
        "down_t": down.reshape(D, J, 128).transpose(2, 1, 0).reshape(128, J * D),
    }
    nc = _bacc.Bacc("TRN2", target_bir_lowering=False, num_devices=1)
    arrays, args = {}, []
    for name, a in laid.items():
        a = _np.ascontiguousarray(a)
        arrays[f"in_{name}_dram"] = a
        args.append(nc.dram_tensor(f"in_{name}_dram", a.shape, _mybir.dt.from_np(a.dtype), kind="ExternalInput").ap())
    args.append(nc.dram_tensor("out_0_dram", rows.shape, _mybir.dt.float32, kind="ExternalOutput").ap())
    bass_cond_norm_geglu_bitlinear(nc, *args)
    r = _run(nc, [arrays], core_ids=[0])
    return r.results[0]["out_0_dram"].reshape(x.shape)
```

```python
from contextlib import ExitStack

import concourse.bass as bass
from concourse import mybir

P = 128
ALU = mybir.AluOpType
ACT = mybir.ActivationFunctionType
F32 = mybir.dt.float32
I32 = mybir.dt.int32
FP16 = mybir.dt.float16
BF16 = mybir.dt.bfloat16
AX = mybir.AxisListType
RADD = bass.bass_isa.ReduceOp.add
RMAX = bass.bass_isa.ReduceOp.max

ROUND = 1.5 * 2.0 ** 23
EXPONENT = 0x7F800000
RSQRT_SEED = 0x5F3759DF
W_TOP = 2.0 ** 14
X_TOP = 2.0 ** 10
EPS = 1e-6
QMAX = 127.0
CLIP = 1e-5


def bass_cond_norm_geglu_bitlinear(
    nc: bass.Bass,
    x_rows: bass.AP,
    x_cols: bass.AP,
    cond_t: bass.AP,
    norm_t: bass.AP,
    up_t: bass.AP,
    down_t: bass.AP,
    out: bass.AP,
):
    T, D = x_rows.shape
    NB, _, cols = x_cols.shape
    C, B = cond_t.shape
    J = up_t.shape[0]
    KT = D // P
    TB = T // NB
    TT = TB // P
    WJ = 2 * KT * P
    PER_B = NB // B
    DC = WJ // D
    ND = J // DC
    WS = 4
    XS = 3
    assert C == P and TB == 512 and D == 512 and cols == KT * TB and J == 16 and WJ == DC * D

    x_rows = x_rows.rearrange("(b p i) d -> b p (i d)", p=P, i=TT)
    out = out.rearrange("(b p i) d -> b p (i d)", p=P, i=TT)

    ds = bass.ds

    with ExitStack() as ctx:
        def sb(name, shape, dt):
            return ctx.enter_context(nc.sbuf_tensor(name, shape, dt))

        def sem(name):
            return ctx.enter_context(nc.semaphore(name))

        w_hi = sb("w_hi", [P, J * WJ], FP16)
        w_lo = sb("w_lo", [P, J * WJ], FP16)
        w_unscale = sb("w_unscale", [P, J], F32)
        dw = sb("dw", [P, J * D], BF16)
        w_raw = sb("w_raw", [P, WS, WJ], F32)
        xt_raw = sb("xt_raw", [P, KT * TB], F32)
        xr = sb("xr", [P, XS * TT * D], F32)
        xn = sb("xn", [P, 2, TB], F32)
        x_hi = sb("x_hi", [P, 2 * KT * TB], FP16)
        x_lo = sb("x_lo", [P, 2 * KT * TB], FP16)
        g = sb("g", [P, 2, TB], F32)
        h = sb("h", [P, J * TB], F32)
        h_max = sb("h_max", [P, TB], F32)
        scaled = sb("scaled", [P, 2, TB], F32)
        q = sb("q", [P, J * TB], BF16)
        sum_junk = q[:, 0:2 * WJ]
        square_junk = [q[:, 2 * WJ + k * TT * D:2 * WJ + (k + 1) * TT * D] for k in range(2)]
        square_junk.append(w_raw[:, 0, :].bitcast(BF16))
        down_sum_raw = xr[:, 2 * TT * D:3 * TT * D].rearrange("p (s n) -> p s n", s=2)
        cond_sb = sb("cond_sb", [P, B], F32)
        norm_sb = scaled[:, 0, :]
        cs_raw = sb("cs_raw", [P, KT * B], F32)
        cs = sb("cs", [P, KT * B], F32)
        cs_unscale = sb("cs_unscale", [P, 1], F32)
        peak = sb("peak", [P, 2], F32)
        peak_all = sb("peak_all", [P, 2], F32)
        p2 = sb("p2", [P, 2], F32)
        p2_inv = sb("p2_inv", [P, 2], F32)
        w_scale = sb("w_scale", [P, 2], F32)
        sumsq = sb("sumsq", [P, TT], F32)
        ms = sb("ms", [P, TT], F32)
        rs = sb("rs", [P, TT], F32)
        rs_t = sb("rs_t", [P, TT], F32)
        row_max = sb("row_max", [P, TT], F32)
        row_rec = sb("row_rec", [P, TT], F32)
        row_scale = sb("row_scale", [P, TT], F32)
        dequant = sb("dequant", [P, TT], F32)
        d_sums = sb("d_sums", [P, ND], F32)
        d_sum = sb("d_sum", [P, 1], F32)
        d_total = sb("d_total", [P, 1], F32)
        d_mean = sb("d_mean", [P, 1], F32)
        d_scale = sb("d_scale", [P, 1], F32)
        ident = sb("ident", [P, P], F32)

        ps_u = ctx.enter_context(nc.psum_tensor("ps_u", [P, 4, 512], F32))
        ps_y = ctx.enter_context(nc.psum_tensor("ps_y", [P, 2, 512], F32))
        ps_m = ctx.enter_context(nc.psum_tensor("ps_m", [P, 512], F32))
        ps_s = ctx.enter_context(nc.psum_tensor("ps_s", [P, 512], F32))

        consts_loaded = sem("consts_loaded")
        ident_ready = sem("ident_ready")
        up_loaded = [sem(f"up_loaded{k}") for k in range(WS)]
        down_sum_loaded = [sem("down_sum_loaded0"), sem("down_sum_loaded1")]
        down_loaded = [sem(f"down_loaded{k}") for k in range(WS)]
        xt_loaded = sem("xt_loaded")
        xr_loaded = sem("xr_loaded")
        y_stored = sem("y_stored")
        cs_matmul = sem("cs_matmul")
        cs_step = sem("cs_step")
        cs_peak = sem("cs_peak")
        cs_peak_all = sem("cs_peak_all")
        w_peak = sem("w_peak")
        w_peak_all = sem("w_peak_all")
        w_step = sem("w_step")
        w_scaled = sem("w_scaled")
        w_hi_ready = sem("w_hi_ready")
        w_ready = sem("w_ready")
        d_summed = sem("d_summed")
        d_sum_ready = sem("d_sum_ready")
        d_total_ready = sem("d_total_ready")
        d_step = sem("d_step")
        d_scale_ready = sem("d_scale_ready")
        d_pass = sem("d_pass")
        dw_ready = sem("dw_ready")
        sumsq_ready = sem("sumsq_ready")
        rs_step = sem("rs_step")
        rs_ready = sem("rs_ready")
        rs_rows = sem("rs_rows")
        xn_ready = sem("xn_ready")
        x_hi_ready = sem("x_hi_ready")
        x_lo_ready = sem("x_lo_ready")
        val_ready = sem("val_ready")
        gate_ready = sem("gate_ready")
        g_ready = sem("g_ready")
        h_abs_ready = sem("h_abs_ready")
        h_ready = sem("h_ready")
        h_max_ready = sem("h_max_ready")
        max_rows = sem("max_rows")
        row_step = sem("row_step")
        scale_ready = sem("scale_ready")
        dequant_ready = sem("dequant_ready")
        scale_rows = sem("scale_rows")
        scaled_ready = sem("scaled_ready")
        q_ready = sem("q_ready")
        y_ready = sem("y_ready")
        y_done = sem("y_done")

        SUM_AT = (0, 1, 2, 4, 6, 8, 10, 11)
        RS_STEPS = 11

        block = ctx.enter_context(nc.Block())

        @block.sync
        def _(sp):
            def load_up(j, slot):
                sp.dma_start(w_raw[:, slot, :], up_t[j]).then_inc(up_loaded[slot], 16)

            def load_down(chunk, to, loaded):
                sp.dma_start(to, down_t[:, ds(chunk * WJ, WJ)]).then_inc(loaded, 16)

            def load_x(b):
                if not isinstance(b, int) or b >= 1:
                    sp.wait_ge(xn_ready, b * KT)
                sp.dma_start(xt_raw[:], x_cols[b]).then_inc(xt_loaded, 16)
                load_x_rows(b)

            def load_x_rows(b):
                if isinstance(b, int) and b == XS - 1:
                    sp.wait_ge(d_summed, ND)
                if not isinstance(b, int) or b >= XS:
                    sp.wait_ge(y_stored, (b - XS + 1) * TT * 16)
                sp.dma_start(xr[:, ds((b % XS) * (TT * D), TT * D)], x_rows[b]).then_inc(xr_loaded, 16)

            def store_y(b):
                for i in range(TT):
                    sp.wait_ge(y_done, b * TT + i + 1)
                    sp.dma_start(out[b][:, i * D:(i + 1) * D], xr[:, ds((b % XS) * (TT * D) + i * D, D)]).then_inc(y_stored, 16)

            sp.dma_start(cond_sb[:], cond_t).then_inc(consts_loaded, 16)
            sp.dma_start(norm_sb, norm_t).then_inc(consts_loaded, 16)
            load_x_rows(0)
            load_up(0, 0)
            sp.dma_start(xt_raw[:], x_cols[0]).then_inc(xt_loaded, 16)
            for j in range(1, WS):
                load_up(j, j)
            for c in range(2):
                load_down(c, down_sum_raw[:, c, :], down_sum_loaded[c])
            load_x(1)
            with sp.Fori(1, J // WS) as i:
                for k in range(WS):
                    sp.wait_ge(w_ready, WS * i + k - WS + 1)
                    load_up(WS * i + k, k)
                    if k % 2 == 1:
                        c = k // 2
                        sp.wait_ge(d_summed, 2 * i + c - 1)
                        load_down(2 * i + c, down_sum_raw[:, c, :], down_sum_loaded[c])
            load_x(2)
            for c in range(ND):
                if c < WS:
                    sp.wait_ge(w_ready, J - WS + c + 1)
                else:
                    sp.wait_ge(dw_ready, c - WS + 1)
                load_down(c, w_raw[:, c % WS, :], down_loaded[c % WS])
            store_y(0)
            with sp.Fori(XS, NB) as b:
                load_x(b)
                store_y(b - 2)
            store_y(NB - 2)
            store_y(NB - 1)
            sp.wait_ge(y_stored, NB * TT * 16)

        @block.tensor
        def _(pe):
            def up_half(b, j, s, which, as_ready=False):
                bank = ps_u[:, 2 * s + which, :]
                done = (val_ready, gate_ready)[which]
                for kt in range(KT):
                    if as_ready:
                        pe.wait_ge(x_hi_ready, b * KT + kt + 1)
                        pe.wait_ge(x_lo_ready, b * KT + kt + 1)
                    w_at = ds(j * WJ + (which * KT + kt) * P, P)
                    x_at = ds((b % 2) * (KT * TB) + kt * TB, TB)
                    pe.matmul(bank, w_hi[:, w_at], x_hi[:, x_at], start=(kt == 0), stop=False)
                    pe.matmul(bank, w_hi[:, w_at], x_lo[:, x_at], start=False, stop=False)
                    last = pe.matmul(bank, w_lo[:, w_at], x_hi[:, x_at], start=False, stop=(kt == KT - 1))
                last.then_inc(done, 1)

            def gate(b, j, s, first=False, prep=False, as_ready=False):
                n = b * J + j
                if prep:
                    pe.wait_ge(w_ready, j + 1)
                if not first:
                    pe.wait_ge(g_ready, n - 1)
                up_half(b, j, s, 1, as_ready)

            def val(b, j, s, first=False):
                n = b * J + j
                if not first:
                    pe.wait_ge(h_ready, n - 1)
                up_half(b, j, s, 0)

            def turn_max(b):
                pe.wait_ge(h_max_ready, (b + 1) * J)
                if not isinstance(b, int) or b < NB - 1:
                    pe.wait_ge(xn_ready, (b + 2) * KT)
                else:
                    pe.wait_ge(xn_ready, NB * KT)
                for i in range(TT):
                    last = pe.transpose(ps_m[:, i * P:(i + 1) * P], h_max[:, i * P:(i + 1) * P], ident[:])
                last.then_inc(max_rows, 1)

            def spread_scale(b):
                pe.wait_ge(scale_ready, b + 1)
                for i in range(TT):
                    last = pe.transpose(ps_s[:, i * P:(i + 1) * P], row_scale[:, i:i + 1].to_broadcast([P, P]), ident[:])
                last.then_inc(scale_rows, 1)

            def spread_rs(b):
                pe.wait_ge(rs_ready, b + 1)
                if not isinstance(b, int) or b >= 2:
                    pe.wait_ge(scale_ready, b - 1)
                for i in range(TT):
                    last = pe.transpose(ps_m[:, i * P:(i + 1) * P], rs[:, i:i + 1].to_broadcast([P, P]), ident[:])
                last.then_inc(rs_rows, 1)

            def down(b, i):
                if i >= 2:
                    pe.wait_ge(y_done, b * TT + i - 1)
                for j in range(J):
                    last = pe.matmul(ps_y[:, i % 2, :], q[:, j * TB + i * P:j * TB + (i + 1) * P],
                                     dw[:, j * D:(j + 1) * D], start=(j == 0), stop=(j == J - 1))
                last.then_inc(y_ready, 1)

            def up_block(b, first=False, last=False):
                gate(b, 0, 0, first, first, as_ready=True)
                if not first:
                    turn_max(b - 1)
                val(b, 0, 0, first)
                if not first:
                    spread_scale(b - 1)
                gate(b, 1, 1, first, first)
                val(b, 1, 1, first)
                with pe.Fori(1, 4) as i:
                    for s in range(2):
                        gate(b, 2 * i + s, s, prep=first)
                        val(b, 2 * i + s, s)
                if not last:
                    spread_rs(b + 1)
                if not first:
                    pe.wait_ge(q_ready, b * J)
                    pe.wait_ge(dw_ready, ND)
                for i in range(4):
                    gate(b, 8 + i, i % 2, prep=first)
                    val(b, 8 + i, i % 2)
                    if not first:
                        down(b - 1, i)
                with pe.Fori(6, 8) as i:
                    for s in range(2):
                        gate(b, 2 * i + s, s, prep=first)
                        val(b, 2 * i + s, s)

            pe.wait_ge(consts_loaded, 32)
            for kt in range(KT):
                last = pe.matmul(ps_y[:, 0, kt * B:(kt + 1) * B], norm_sb[:, kt * P:(kt + 1) * P], cond_sb[:],
                                 start=True, stop=True)
            last.then_inc(cs_matmul, 1)
            pe.wait_ge(ident_ready, 1)
            spread_rs(0)
            up_block(0, first=True)
            with pe.Fori(1, NB - 1) as b:
                up_block(b)
            up_block(NB - 1, last=True)
            turn_max(NB - 1)
            spread_scale(NB - 1)
            pe.wait_ge(h_ready, NB * J)
            for j in range(J):
                pe.wait_ge(q_ready, (NB - 1) * J + j + 1)
                for i in range(TT):
                    last = pe.matmul(ps_u[:, i, :], q[:, j * TB + i * P:j * TB + (i + 1) * P],
                                     dw[:, j * D:(j + 1) * D], start=(j == 0), stop=(j == J - 1))
                    if j == J - 1:
                        last.then_inc(y_ready, 1)

        @block.scalar
        def _(act):
            def gelu(b, j, s, first=False):
                n = b * J + j
                act.wait_ge(gate_ready, n + 1)
                if first:
                    act.wait_ge(w_scaled, 2)
                else:
                    act.wait_ge(h_max_ready, n - 1)
                act.activation(g[:, s, :], ps_u[:, 2 * s + 1, :], ACT.Gelu,
                               scale=w_unscale[:, ds(j, 1)]).then_inc(g_ready, 1)

            def absolute(b, j, s):
                act.wait_ge(h_ready, b * J + j + 1)
                act.activation(g[:, s, :], h[:, ds(j * TB, TB)], ACT.Abs).then_inc(h_abs_ready, 1)

            def squares(b):
                act.wait_ge(xr_loaded, (b + 1) * 16)
                if not isinstance(b, int) or b >= 1:
                    act.wait_ge(rs_ready, b)
                junk = square_junk[b if isinstance(b, int) and b <= 1 else 2]
                if not isinstance(b, int) or b >= 2:
                    act.wait_ge(dw_ready, ND - WS + 1)
                for i in range(TT):
                    last = act.activation(junk[:, i * D:(i + 1) * D], xr[:, ds((b % XS) * (TT * D) + i * D, D)], ACT.Square,
                                          accum_out=sumsq[:, i:i + 1])
                last.then_inc(sumsq_ready, 1)

            def high(b, kt):
                act.wait_ge(xn_ready, b * KT + kt + 1)
                if not isinstance(b, int) or b >= 2:
                    act.wait_ge(val_ready, (b - 1) * J)
                act.copy(x_hi[:, ds((b % 2) * (KT * TB) + kt * TB, TB)], xn[:, kt % 2, :]).then_inc(x_hi_ready, 1)

            def weight_high(j, slot):
                act.wait_ge(w_scaled, j + 1)
                act.activation(w_hi[:, ds(j * WJ, WJ)], w_raw[:, j % WS, :], ACT.Copy,
                               scale=w_scale[:, slot:slot + 1]).then_inc(w_hi_ready, 1)

            def sum_down(chunk, slot):
                act.wait_ge(down_sum_loaded[slot], (chunk // 2 + 1) * 16)
                if not isinstance(chunk, int) or chunk >= 2:
                    act.wait_ge(d_summed, chunk - 1)
                act.activation(sum_junk[:, slot * WJ:(slot + 1) * WJ], down_sum_raw[:, slot, :], ACT.Abs,
                               accum_out=d_sums[:, ds(chunk, 1)]).then_inc(d_summed, 1)

            squares(0)
            weight_high(0, 0)
            for kt in range(KT):
                high(0, kt)
            weight_high(1, 1)
            for j in range(J):
                if j + 2 < J:
                    weight_high(j + 2, j % 2)
                gelu(0, j, j % 2, first=j < 2)
                absolute(0, j, j % 2)
                if j in SUM_AT:
                    sum_down(SUM_AT.index(j), SUM_AT.index(j) % 2)
                if j == 5:
                    squares(1)
                if 8 <= j < 8 + KT:
                    high(1, j - 8)

            def pair(b, j, s):
                gelu(b, j, s)
                absolute(b, j, s)

            def up_block(b, last=False):
                with act.Fori(0, 2) as i:
                    for s in range(2):
                        pair(b, 2 * i + s, s)
                if not last:
                    squares(b + 1)
                with act.Fori(2, 4) as i:
                    for s in range(2):
                        pair(b, 2 * i + s, s)
                for k in range(4):
                    pair(b, 8 + k, k % 2)
                    if not last:
                        high(b + 1, k)
                with act.Fori(6, 8) as i:
                    for s in range(2):
                        pair(b, 2 * i + s, s)

            with act.Fori(1, NB - 1) as b:
                up_block(b)
            up_block(NB - 1, last=True)

        @block.gpsimd
        def _(pool):
            pool.memset(ident[:], 0.0).then_inc(ident_ready, 1)
            pool.wait_ge(ident_ready, 1)
            pool.affine_select(out=ident[:], in_=ident[:], compare_op=ALU.not_equal, fill=1.0, base=0,
                               pattern=[[-1, P]], channel_multiplier=1).then_inc(ident_ready, 1)
            pool.wait_ge(cs_peak, 1)
            pool.partition_all_reduce(peak_all[:, 0:1], peak[:, 0:1], P, RMAX).then_inc(cs_peak_all, 1)
            for j in range(J):
                s = j % 2
                pool.wait_ge(w_peak, j + 1)
                pool.partition_all_reduce(peak_all[:, s:s + 1], peak[:, s:s + 1], P, RMAX).then_inc(w_peak_all, 1)
                if j == J - 2:
                    pool.wait_ge(d_sum_ready, 1)
                    pool.partition_all_reduce(d_total[:], d_sum[:], P, RADD).then_inc(d_total_ready, 1)
            pool.wait_ge(d_scale_ready, 1)
            for i in range(ND // 2):
                for s in range(2):
                    c = 2 * i + s
                    raw = w_raw[:, c % WS, :]
                    pool.wait_ge(down_loaded[c % WS], (c // WS + 1) * 16)
                    pool.tensor_scalar(raw, raw, d_scale[:], ROUND, ALU.mult, ALU.add).then_inc(d_pass, 1)
                    pool.wait_ge(d_pass, 2 * c + 1)
                    pool.tensor_scalar(raw, raw, -ROUND, 1.0, ALU.add, ALU.mult).then_inc(d_pass, 1)
                    pool.wait_ge(d_pass, 2 * c + 2)
                    pool.tensor_scalar(dw[:, ds(c * WJ, WJ)], raw, 1.0, -1.0, ALU.min, ALU.max).then_inc(dw_ready, 1)

        @block.vector
        def _(dve):
            def weight_peak(j, slot):
                dve.wait_ge(up_loaded[j % WS], (j // WS + 1) * 16)
                if not isinstance(j, int) or j >= 2:
                    dve.wait_ge(w_peak_all, j - 1)
                dve.tensor_reduce(peak[:, slot:slot + 1], w_raw[:, j % WS, :], AX.X, ALU.max,
                                  apply_absolute_value=True).then_inc(w_peak, 1)

            def power_of_two(slot, step, count):
                a, p, pi = peak_all[:, slot:slot + 1], p2[:, slot:slot + 1], p2_inv[:, slot:slot + 1]
                dve.tensor_scalar(a, a, 2.0 ** -100, 2.0 ** 110, ALU.max, ALU.min).then_inc(step, 1)
                dve.wait_ge(step, count + 1)
                dve.tensor_scalar(p.bitcast(I32), a.bitcast(I32), EXPONENT, None, ALU.bitwise_and).then_inc(step, 1)
                dve.wait_ge(step, count + 2)
                dve.reciprocal(pi, p).then_inc(step, 1)
                dve.wait_ge(step, count + 3)

            def weight_scale(j, slot):
                dve.wait_ge(w_peak_all, j + 1)
                power_of_two(slot, w_step, 4 * j)
                dve.tensor_scalar(w_unscale[:, ds(j, 1)], p2[:, slot:slot + 1], cs_unscale[:], None,
                                  ALU.mult).then_inc(w_step, 1)
                dve.wait_ge(w_step, 4 * j + 4)
                dve.tensor_scalar(w_scale[:, slot:slot + 1], p2_inv[:, slot:slot + 1], W_TOP, None,
                                  ALU.mult).then_inc(w_scaled, 1)

            def weight_low(j, slot):
                dve.wait_ge(w_scaled, j + 1)
                dve.wait_ge(w_hi_ready, j + 1)
                at = ds(j * WJ, WJ)
                dve.scalar_tensor_tensor(out=w_lo[:, at], in0=w_raw[:, j % WS, :], scalar=w_scale[:, slot:slot + 1],
                                         in1=w_hi[:, at], op0=ALU.mult, op1=ALU.subtract).then_inc(w_ready, 1)

            def rsqrt(b):
                base = b * RS_STEPS
                dve.wait_ge(sumsq_ready, b + 1)
                if not isinstance(b, int) or b >= 1:
                    dve.wait_ge(rs_rows, b)
                dve.tensor_scalar(ms[:], sumsq[:], 1.0 / D, EPS, ALU.mult, ALU.add).then_inc(rs_step, 1)
                dve.wait_ge(rs_step, base + 1)
                dve.tensor_scalar(rs_t[:].bitcast(I32), ms[:].bitcast(I32), 1, None,
                                  ALU.logical_shift_right).then_inc(rs_step, 1)
                dve.wait_ge(rs_step, base + 2)
                dve.tensor_scalar(rs[:].bitcast(I32), rs_t[:].bitcast(I32), -1.0, float(RSQRT_SEED),
                                  ALU.mult, ALU.add).then_inc(rs_step, 1)
                dve.wait_ge(rs_step, base + 3)
                for k in range(3):
                    dve.tensor_tensor(rs_t[:], rs[:], rs[:], ALU.mult).then_inc(rs_step, 1)
                    dve.wait_ge(rs_step, base + 3 * k + 4)
                    dve.scalar_tensor_tensor(out=rs_t[:], in0=rs_t[:], scalar=-0.5, in1=ms[:],
                                             op0=ALU.mult, op1=ALU.mult).then_inc(rs_step, 1)
                    dve.wait_ge(rs_step, base + 3 * k + 5)
                    last = dve.scalar_tensor_tensor(out=rs[:], in0=rs_t[:], scalar=1.5, in1=rs[:],
                                                    op0=ALU.add, op1=ALU.mult)
                    if k < 2:
                        last.then_inc(rs_step, 1)
                        dve.wait_ge(rs_step, base + 3 * k + 6)
                    else:
                        last.then_inc(rs_ready, 1)

            def norm(b, kt):
                dve.wait_ge(rs_rows, b + 1)
                dve.wait_ge(xt_loaded, (b + 1) * 16)
                if kt >= 2:
                    dve.wait_ge(x_lo_ready, b * KT + kt - 1)
                elif not isinstance(b, int) or b >= 1:
                    dve.wait_ge(x_lo_ready, b * KT + kt - 1)
                dve.scalar_tensor_tensor(out=xn[:, kt % 2, :], in0=xt_raw[:, kt * TB:(kt + 1) * TB],
                                         scalar=cs[:, ds(kt * B + b // PER_B, 1)], in1=ps_m[:],
                                         op0=ALU.mult, op1=ALU.mult).then_inc(xn_ready, 1)

            def low(b, kt):
                at = ds((b % 2) * (KT * TB) + kt * TB, TB)
                dve.wait_ge(x_hi_ready, b * KT + kt + 1)
                dve.tensor_tensor(x_lo[:, at], xn[:, kt % 2, :], x_hi[:, at], ALU.subtract).then_inc(x_lo_ready, 1)

            def hidden(b, j, s, first=False):
                n = b * J + j
                at = ds(j * TB, TB)
                dve.wait_ge(val_ready, n + 1)
                dve.wait_ge(g_ready, n + 1)
                if not first:
                    dve.wait_ge(scaled_ready, n - J + 1)
                dve.scalar_tensor_tensor(out=h[:, at], in0=ps_u[:, 2 * s, :], scalar=w_unscale[:, ds(j, 1)],
                                         in1=g[:, s, :], op0=ALU.mult, op1=ALU.mult).then_inc(h_ready, 1)

            def peak_of(b, j, s, first=False):
                n = b * J + j
                dve.wait_ge(h_abs_ready, n + 1)
                if isinstance(j, int) and j == 0:
                    if not first:
                        dve.wait_ge(max_rows, b)
                    dve.tensor_copy(h_max[:], g[:, s, :]).then_inc(h_max_ready, 1)
                else:
                    dve.wait_ge(h_max_ready, n)
                    dve.tensor_tensor(h_max[:], g[:, s, :], h_max[:], ALU.max).then_inc(h_max_ready, 1)

            def row_scales(b):
                dve.wait_ge(max_rows, b + 1)
                dve.tensor_reduce(row_max[:], ps_m[:].rearrange("p (i n) -> p i n", i=TT), AX.X,
                                  ALU.max).then_inc(row_step, 1)
                dve.wait_ge(row_step, 3 * b + 1)
                dve.tensor_scalar(row_max[:], row_max[:], CLIP, None, ALU.max).then_inc(row_step, 1)
                dve.wait_ge(row_step, 3 * b + 2)
                dve.reciprocal(row_rec[:], row_max[:]).then_inc(row_step, 1)
                dve.wait_ge(row_step, 3 * b + 3)
                dve.tensor_scalar(row_scale[:], row_rec[:], QMAX, None, ALU.mult).then_inc(scale_ready, 1)
                dve.tensor_scalar(dequant[:], row_max[:], 1.0 / QMAX, d_mean[:], ALU.mult,
                                  ALU.mult).then_inc(dequant_ready, 1)

            def quantize(b, t):
                for s in range(2):
                    m = b * J + t + s
                    if isinstance(t, int) and t == 0:
                        dve.wait_ge(scale_rows, b + 1)
                    if not (isinstance(t, int) and t == 0):
                        dve.wait_ge(q_ready, m - 1)
                    dve.tensor_tensor(scaled[:, s, :], h[:, ds((t + s) * TB, TB)], ps_s[:],
                                      ALU.mult).then_inc(scaled_ready, 1)
                for s in range(2):
                    m = b * J + t + s
                    dve.wait_ge(scaled_ready, m + 1)
                    dve.tensor_scalar(q[:, ds((t + s) * TB, TB)], scaled[:, s, :], ROUND, ROUND, ALU.add,
                                      ALU.subtract).then_inc(q_ready, 1)

            def residual(b, i, bank):
                at = ds((b % XS) * (TT * D) + i * D, D)
                dve.wait_ge(y_ready, b * TT + i + 1)
                dve.wait_ge(dequant_ready, b + 1)
                dve.scalar_tensor_tensor(out=xr[:, at], in0=bank, scalar=dequant[:, i:i + 1], in1=xr[:, at],
                                         op0=ALU.mult, op1=ALU.add).then_inc(y_done, 1)

            dve.wait_ge(cs_matmul, 1)
            dve.tensor_scalar(cs_raw[:], ps_y[:, 0, 0:KT * B], 1.0, None, ALU.add).then_inc(cs_step, 1)
            dve.wait_ge(cs_step, 1)
            dve.tensor_reduce(peak[:, 0:1], cs_raw[:], AX.X, ALU.max, apply_absolute_value=True).then_inc(cs_peak, 1)
            dve.wait_ge(cs_peak_all, 1)
            power_of_two(0, cs_step, 1)
            dve.tensor_scalar(cs_unscale[:], p2[:, 0:1], 1.0 / (W_TOP * X_TOP), None, ALU.mult).then_inc(cs_step, 1)
            dve.tensor_scalar(cs[:], cs_raw[:], p2_inv[:, 0:1], X_TOP, ALU.mult, ALU.mult).then_inc(cs_step, 1)
            dve.wait_ge(cs_step, 6)
            weight_peak(0, 0)
            rsqrt(0)
            weight_scale(0, 0)
            norm(0, 0)
            weight_peak(1, 1)
            weight_low(0, 0)
            low(0, 0)
            norm(0, 1)
            norm(0, 2)
            low(0, 1)
            low(0, 2)
            norm(0, 3)
            weight_scale(1, 1)
            low(0, 3)
            weight_peak(2, 0)
            weight_low(1, 1)
            for j in range(J):
                if j + 2 < J:
                    weight_scale(j + 2, j % 2)
                if j + 3 < J:
                    weight_peak(j + 3, (j + 1) % 2)
                if j + 2 < J:
                    weight_low(j + 2, j % 2)
                if j >= 1:
                    peak_of(0, j - 1, (j - 1) % 2, first=True)
                hidden(0, j, j % 2, first=True)
                if j == 6:
                    rsqrt(1)
                if j == SUM_AT[-1]:
                    dve.wait_ge(d_summed, ND)
                    dve.tensor_reduce(d_sum[:], d_sums[:], AX.X, ALU.add).then_inc(d_sum_ready, 1)
                if 8 <= j < 8 + KT:
                    norm(1, j - 8)
                    low(1, j - 8)
                if j == J - 2:
                    dve.wait_ge(d_total_ready, 1)
                    dve.tensor_scalar(d_mean[:], d_total[:], 1.0 / (J * P * D), CLIP, ALU.mult,
                                      ALU.max).then_inc(d_step, 1)
                    dve.wait_ge(d_step, 1)
                    dve.reciprocal(d_scale[:], d_mean[:]).then_inc(d_scale_ready, 1)
            peak_of(0, J - 1, (J - 1) % 2, first=True)

            def up_block(b, last=False):
                row_scales(b - 1)
                quantize(b - 1, 0)
                hidden(b, 0, 0)
                quantize(b - 1, 2)
                peak_of(b, 0, 0)
                hidden(b, 1, 1)
                quantize(b - 1, 4)
                peak_of(b, 1, 1)
                with dve.Fori(1, 3) as i:
                    for s in range(2):
                        hidden(b, 2 * i + s, s)
                        quantize(b - 1, 4 * i + 2 * s + 2)
                        peak_of(b, 2 * i + s, s)
                if not last:
                    rsqrt(b + 1)
                hidden(b, 6, 0)
                quantize(b - 1, J - 2)
                peak_of(b, 6, 0)
                hidden(b, 7, 1)
                peak_of(b, 7, 1)
                for k in range(4):
                    hidden(b, 8 + k, k % 2)
                    if not last:
                        norm(b + 1, k)
                        low(b + 1, k)
                    peak_of(b, 8 + k, k % 2)
                    residual(b - 1, k, ps_y[:, k % 2, :])
                with dve.Fori(6, 8) as i:
                    for s in range(2):
                        hidden(b, 2 * i + s, s)
                        peak_of(b, 2 * i + s, s)

            with dve.Fori(1, NB - 1) as b:
                up_block(b)
            up_block(NB - 1, last=True)
            row_scales(NB - 1)
            for t in range(0, J, 2):
                quantize(NB - 1, t)
            for i in range(TT):
                residual(NB - 1, i, ps_u[:, i, :])


def kernel(x, cond_256, L0_cond_norm_w, L0_cond_up_w, L0_cond_down_w):
    import numpy as _np
    import concourse.bacc as _bacc
    from concourse import mybir as _mybir
    from concourse.bass_utils import run_bass_kernel_spmd as _run

    x = _np.asarray(x)
    up, down = _np.asarray(L0_cond_up_w), _np.asarray(L0_cond_down_w)
    S0, S1, D = x.shape
    FF = down.shape[1]
    TB, KT, J = 512, D // 128, FF // 128
    rows = x.reshape(S0 * S1, D)
    laid = {
        "x_rows": rows,
        "x_cols": rows.reshape(-1, 128, TB // 128, KT, 128).transpose(0, 4, 3, 2, 1).reshape(-1, 128, KT * TB),
        "cond_t": _np.asarray(cond_256).T,
        "norm_t": _np.asarray(L0_cond_norm_w).T,
        "up_t": up.reshape(2, J, 128, KT, 128).transpose(1, 4, 0, 3, 2).reshape(J, 128, 2 * KT * 128),
        "down_t": down.reshape(D, J, 128).transpose(2, 1, 0).reshape(128, J * D),
    }
    nc = _bacc.Bacc("TRN2", target_bir_lowering=False, num_devices=1)
    arrays, args = {}, []
    for name, a in laid.items():
        a = _np.ascontiguousarray(a)
        arrays[f"in_{name}_dram"] = a
        args.append(nc.dram_tensor(f"in_{name}_dram", a.shape, _mybir.dt.from_np(a.dtype), kind="ExternalInput").ap())
    args.append(nc.dram_tensor("out_0_dram", rows.shape, _mybir.dt.float32, kind="ExternalOutput").ap())
    bass_cond_norm_geglu_bitlinear(nc, *args)
    r = _run(nc, [arrays], core_ids=[0])
    return r.results[0]["out_0_dram"].reshape(x.shape)
```

```python
import math
from contextlib import ExitStack

import concourse.bass as bass
from concourse import mybir

P = 128
ALU = mybir.AluOpType
ACT = mybir.ActivationFunctionType
F32 = mybir.dt.float32
I32 = mybir.dt.int32
FP16 = mybir.dt.float16
BF16 = mybir.dt.bfloat16
AX = mybir.AxisListType
RADD = bass.bass_isa.ReduceOp.add
RMAX = bass.bass_isa.ReduceOp.max

ROUND = 1.5 * 2.0 ** 23
EXPONENT = 0x7F800000
RSQRT_SEED = 0x5F3759DF
W_TOP = 2.0 ** 14
X_TOP = 2.0 ** 10
EPS = 1e-6
QMAX = 127.0
CLIP = 1e-5


def bass_cond_norm_geglu_bitlinear(
    nc: bass.Bass,
    x_rows: bass.AP,
    x_cols: bass.AP,
    cond_t: bass.AP,
    norm_t: bass.AP,
    up_t: bass.AP,
    down_t: bass.AP,
    out: bass.AP,
):
    T, D = x_rows.shape
    NB, _, cols = x_cols.shape
    C, B = cond_t.shape
    J = up_t.shape[0]
    KT = D // P
    TB = T // NB
    TT = TB // P
    WJ = 2 * KT * P
    PER_B = NB // B
    DC = WJ // D
    ND = J // DC
    WS = 4
    XS = 3
    assert C == P and TB == 512 and D == 512 and cols == KT * TB and J == 16 and WJ == DC * D

    x_rows = x_rows.rearrange("(b p i) d -> b p (i d)", p=P, i=TT)
    out = out.rearrange("(b p i) d -> b p (i d)", p=P, i=TT)

    ds = bass.ds

    with ExitStack() as ctx:
        def sb(name, shape, dt):
            return ctx.enter_context(nc.sbuf_tensor(name, shape, dt))

        def sem(name):
            return ctx.enter_context(nc.semaphore(name))

        w_hi = sb("w_hi", [P, J * WJ], FP16)
        w_lo = sb("w_lo", [P, J * WJ], FP16)
        w_unscale = sb("w_unscale", [P, J], F32)
        dw = sb("dw", [P, J * D], BF16)
        w_raw = sb("w_raw", [P, WS, WJ], F32)
        xt_raw = sb("xt_raw", [P, KT * TB], F32)
        xr = sb("xr", [P, XS * TT * D], F32)
        xn = sb("xn", [P, 2, TB], F32)
        x_hi = sb("x_hi", [P, 2 * KT * TB], FP16)
        x_lo = sb("x_lo", [P, 2 * KT * TB], FP16)
        g = sb("g", [P, 2, TB], F32)
        h = sb("h", [P, J * TB], F32)
        h_max = sb("h_max", [P, TB], F32)
        scaled = sb("scaled", [P, 2, TB], F32)
        q = sb("q", [P, J * TB], BF16)
        sum_junk = q[:, 0:2 * WJ]
        bound_junk = q[:, 6 * WJ:8 * WJ]
        square_junk = [q[:, 2 * WJ + k * TT * D:2 * WJ + (k + 1) * TT * D] for k in range(2)]
        square_junk.append(w_raw[:, 0, :].bitcast(BF16))
        q_last = w_raw[:].rearrange("p s n -> p (s n)").bitcast(BF16)
        down_sum_raw = xr[:, 2 * TT * D:3 * TT * D].rearrange("p (s n) -> p s n", s=2)
        cond_sb = sb("cond_sb", [P, B], F32)
        norm_sb = scaled[:, 0, :]
        cs_raw = sb("cs_raw", [P, KT * B], F32)
        cs = sb("cs", [P, KT * B], F32)
        cs_unscale = sb("cs_unscale", [P, 1], F32)
        peak = sb("peak", [P, 2], F32)
        peak_all = sb("peak_all", [P, 2], F32)
        p2 = sb("p2", [P, 2], F32)
        cs_scale = sb("cs_scale", [P, 1], F32)
        w_scale = sb("w_scale", [P, 2], F32)
        sumsq = sb("sumsq", [P, TT], F32)
        ms = sb("ms", [P, TT], F32)
        rs = sb("rs", [P, TT], F32)
        rs_t = sb("rs_t", [P, TT], F32)
        row_max = sb("row_max", [P, TT], F32)
        row_rec = sb("row_rec", [P, TT], F32)
        row_scale = sb("row_scale", [P, TT], F32)
        dequant = sb("dequant", [P, TT], F32)
        dequant_last = sb("dequant_last", [P, TT], F32)
        d_sums = sb("d_sums", [P, ND], F32)
        d_sum = sb("d_sum", [P, 1], F32)
        d_total = sb("d_total", [P, 1], F32)
        d_mean = sb("d_mean", [P, 1], F32)
        d_scale = sb("d_scale", [P, 1], F32)
        ident = sb("ident", [P, P], F32)

        ps_u = ctx.enter_context(nc.psum_tensor("ps_u", [P, 4, 512], F32))
        ps_y = ctx.enter_context(nc.psum_tensor("ps_y", [P, 2, 512], F32))
        ps_m = ctx.enter_context(nc.psum_tensor("ps_m", [P, 512], F32))
        ps_s = ctx.enter_context(nc.psum_tensor("ps_s", [P, 512], F32))

        consts_loaded = sem("consts_loaded")
        ident_ready = sem("ident_ready")
        up_loaded = [sem(f"up_loaded{k}") for k in range(WS)]
        down_sum_loaded = [sem("down_sum_loaded0"), sem("down_sum_loaded1")]
        down_loaded = [sem(f"down_loaded{k}") for k in range(WS)]
        xt_loaded = sem("xt_loaded")
        xr_loaded = sem("xr_loaded")
        y_stored = sem("y_stored")
        cs_matmul = sem("cs_matmul")
        cs_step = sem("cs_step")
        cs_peak = sem("cs_peak")
        cs_peak_all = sem("cs_peak_all")
        w_bound = sem("w_bound")
        w_bound_all = sem("w_bound_all")
        w_step = sem("w_step")
        w_scaled = sem("w_scaled")
        w_unscaled = sem("w_unscaled")
        w_hi_ready = sem("w_hi_ready")
        w_ready = sem("w_ready")
        d_summed = sem("d_summed")
        d_sum_ready = sem("d_sum_ready")
        d_total_ready = sem("d_total_ready")
        d_step = sem("d_step")
        d_scale_ready = sem("d_scale_ready")
        d_pass = sem("d_pass")
        dw_ready = sem("dw_ready")
        sumsq_ready = sem("sumsq_ready")
        sumsq_dve_ready = sem("sumsq_dve_ready")
        rs_step = sem("rs_step")
        rs_ready = sem("rs_ready")
        rs_rows = sem("rs_rows")
        xn_ready = sem("xn_ready")
        x_hi_ready = sem("x_hi_ready")
        x_lo_ready = sem("x_lo_ready")
        val_ready = sem("val_ready")
        gate_ready = sem("gate_ready")
        g_ready = sem("g_ready")
        h_abs_ready = sem("h_abs_ready")
        h_ready = sem("h_ready")
        h_max_ready = sem("h_max_ready")
        max_rows = sem("max_rows")
        row_step = sem("row_step")
        scale_ready = sem("scale_ready")
        dequant_ready = sem("dequant_ready")
        scale_rows = sem("scale_rows")
        scaled_ready = sem("scaled_ready")
        q_ready = sem("q_ready")
        round_step = sem("round_step")
        q_act_ready = sem("q_act_ready")
        y_ready = sem("y_ready")
        y_done = sem("y_done")

        RSQRT_AT = 4
        NORM_AT = 8
        SUM_AT = (0, 1, 2, 4, 5, 7, 9, 10)

        RS_STEPS = 11

        block = ctx.enter_context(nc.Block())

        @block.sync
        def _(sp):
            def load_up(j, slot):
                sp.dma_start(w_raw[:, slot, :], up_t[j]).then_inc(up_loaded[slot], 16)

            def load_down(chunk, to, loaded):
                sp.dma_start(to, down_t[:, ds(chunk * WJ, WJ)]).then_inc(loaded, 16)

            def load_x(b):
                if not isinstance(b, int) or b >= 1:
                    sp.wait_ge(xn_ready, b * KT)
                sp.dma_start(xt_raw[:], x_cols[b]).then_inc(xt_loaded, 16)
                load_x_rows(b)

            def load_x_rows(b):
                if isinstance(b, int) and b == XS - 1:
                    sp.wait_ge(d_summed, ND)
                if not isinstance(b, int) or b >= XS:
                    sp.wait_ge(y_stored, (b - XS + 1) * TT * 16)
                sp.dma_start(xr[:, ds((b % XS) * (TT * D), TT * D)], x_rows[b]).then_inc(xr_loaded, 16)

            def store_y(b):
                for i in range(TT):
                    sp.wait_ge(y_done, b * TT + i + 1)
                    sp.dma_start(out[b][:, i * D:(i + 1) * D],
                                 xr[:, ds((b % XS) * (TT * D) + i * D, D)]).then_inc(y_stored, 16)

            sp.dma_start(cond_sb[:], cond_t).then_inc(consts_loaded, 16)
            sp.dma_start(norm_sb, norm_t).then_inc(consts_loaded, 16)
            load_x_rows(0)
            load_up(0, 0)
            sp.dma_start(xt_raw[:], x_cols[0]).then_inc(xt_loaded, 16)
            for j in range(1, WS):
                load_up(j, j)
            for c in range(2):
                load_down(c, down_sum_raw[:, c, :], down_sum_loaded[c])
            load_x(1)
            with sp.Fori(1, J // WS) as i:
                for k in range(WS):
                    sp.wait_ge(w_ready, WS * i + k - WS + 1)
                    load_up(WS * i + k, k)
                    if k % 2 == 1:
                        c = k // 2
                        sp.wait_ge(d_summed, 2 * i + c - 1)
                        load_down(2 * i + c, down_sum_raw[:, c, :], down_sum_loaded[c])
            load_x(2)
            for c in range(ND):
                if c < WS:
                    sp.wait_ge(w_ready, J - WS + c + 1)
                else:
                    sp.wait_ge(dw_ready, c - WS + 1)
                load_down(c, w_raw[:, c % WS, :], down_loaded[c % WS])
            store_y(0)
            with sp.Fori(XS, NB) as b:
                load_x(b)
                store_y(b - 2)
            store_y(NB - 2)
            store_y(NB - 1)
            sp.wait_ge(y_stored, NB * TT * 16)

        @block.tensor
        def _(pe):
            def up_half(b, j, s, which, as_ready=False):
                bank = ps_u[:, 2 * s + which, :]
                done = (val_ready, gate_ready)[which]
                for kt in range(KT):
                    if as_ready:
                        pe.wait_ge(x_hi_ready, b * KT + kt + 1)
                        pe.wait_ge(x_lo_ready, b * KT + kt + 1)
                    w_at = ds(j * WJ + (which * KT + kt) * P, P)
                    x_at = ds((b % 2) * (KT * TB) + kt * TB, TB)
                    pe.matmul(bank, w_hi[:, w_at], x_hi[:, x_at], start=(kt == 0), stop=False)
                    pe.matmul(bank, w_hi[:, w_at], x_lo[:, x_at], start=False, stop=False)
                    last = pe.matmul(bank, w_lo[:, w_at], x_hi[:, x_at], start=False, stop=(kt == KT - 1))
                last.then_inc(done, 1)

            def gate(b, j, s, first=False, prep=False, as_ready=False):
                n = b * J + j
                if prep:
                    pe.wait_ge(w_ready, j + 1)
                if not first:
                    pe.wait_ge(g_ready, n - 1)
                up_half(b, j, s, 1, as_ready)

            def val(b, j, s, first=False):
                n = b * J + j
                if not first:
                    pe.wait_ge(h_ready, n - 1)
                up_half(b, j, s, 0)

            def turn_max(b):
                pe.wait_ge(h_max_ready, (b + 1) * J)
                if not isinstance(b, int) or b < NB - 1:
                    pe.wait_ge(xn_ready, (b + 2) * KT)
                else:
                    pe.wait_ge(xn_ready, NB * KT)
                for i in range(TT):
                    last = pe.transpose(ps_m[:, i * P:(i + 1) * P], h_max[:, i * P:(i + 1) * P], ident[:])
                last.then_inc(max_rows, 1)

            def spread_scale(b):
                pe.wait_ge(scale_ready, b + 1)
                for i in range(TT):
                    last = pe.transpose(ps_s[:, i * P:(i + 1) * P], row_scale[:, i:i + 1].to_broadcast([P, P]), ident[:])
                last.then_inc(scale_rows, 1)

            def spread_rs(b):
                pe.wait_ge(rs_ready, b + 1)
                if not isinstance(b, int) or b >= 2:
                    pe.wait_ge(scale_ready, b - 1)
                for i in range(TT):
                    last = pe.transpose(ps_m[:, i * P:(i + 1) * P], rs[:, i:i + 1].to_broadcast([P, P]), ident[:])
                last.then_inc(rs_rows, 1)

            def down(b, i, js=range(J)):
                if i >= 2 and js[0] == 0:
                    pe.wait_ge(y_done, b * TT + i - 1)
                for j in js:
                    last = pe.matmul(ps_y[:, i % 2, :], q[:, j * TB + i * P:j * TB + (i + 1) * P],
                                     dw[:, j * D:(j + 1) * D], start=(j == 0), stop=(j == J - 1))
                if js[-1] == J - 1:
                    last.then_inc(y_ready, 1)

            def up_block(b, first=False, last=False):
                gate(b, 0, 0, first, first, as_ready=True)
                if not first:
                    turn_max(b - 1)
                val(b, 0, 0, first)
                if not first:
                    spread_scale(b - 1)
                gate(b, 1, 1, first, first)
                val(b, 1, 1, first)
                with pe.Fori(1, 4) as i:
                    for s in range(2):
                        gate(b, 2 * i + s, s, prep=first)
                        val(b, 2 * i + s, s)
                if not (last or first):
                    spread_rs(b + 1)
                if not first:
                    pe.wait_ge(q_ready, b * J)
                    pe.wait_ge(dw_ready, ND)
                for i in range(4):
                    gate(b, 8 + i, i % 2, prep=first)
                    val(b, 8 + i, i % 2)
                    if first and 8 + i == max(8, NORM_AT - 1):
                        spread_rs(b + 1)
                    if not first and not (last and i >= 2):
                        down(b - 1, i)
                with pe.Fori(6, 8) as i:
                    for s in range(2):
                        gate(b, 2 * i + s, s, prep=first)
                        val(b, 2 * i + s, s)

            pe.wait_ge(consts_loaded, 32)
            for kt in range(KT):
                last = pe.matmul(ps_y[:, 0, kt * B:(kt + 1) * B], norm_sb[:, kt * P:(kt + 1) * P], cond_sb[:],
                                 start=True, stop=True)
            last.then_inc(cs_matmul, 1)
            pe.wait_ge(ident_ready, 2)
            spread_rs(0)
            up_block(0, first=True)
            with pe.Fori(1, NB - 1) as b:
                up_block(b)
            up_block(NB - 1, last=True)
            down(NB - 2, 2, range(0, 10))
            turn_max(NB - 1)
            down(NB - 2, 2, range(10, J))
            down(NB - 2, 3, range(0, 5))
            spread_scale(NB - 1)
            down(NB - 2, 3, range(5, J))
            pe.wait_ge(h_ready, NB * J)

            def last_down(j, i):
                return pe.matmul(ps_u[:, i, :], q_last[:, j * TB + i * P:j * TB + (i + 1) * P],
                                 dw[:, j * D:(j + 1) * D], start=(j == 0), stop=(j == J - 1))

            def quantized(j):
                if j % 2 == 0:
                    pe.wait_ge(q_ready, (NB - 1) * J + j // 2 + 1)
                else:
                    pe.wait_ge(q_act_ready, (j + 1) // 2)

            for j in range(J - 4):
                quantized(j)
                for i in range(TT):
                    last_down(j, i)
            for i in range(TT):
                for j in range(J - 4, J):
                    if i == 0:
                        quantized(j)
                    last = last_down(j, i)
                last.then_inc(y_ready, 1)

        @block.scalar
        def _(act):
            def gelu(b, j, s, first=False):
                n = b * J + j
                act.wait_ge(gate_ready, n + 1)
                if isinstance(b, int) and b == 0:
                    act.wait_ge(w_unscaled, j + 1)
                if not first:
                    act.wait_ge(h_max_ready, n - 1)
                act.activation(g[:, s, :], ps_u[:, 2 * s + 1, :], ACT.Gelu,
                               scale=w_unscale[:, ds(j, 1)]).then_inc(g_ready, 1)

            def absolute(b, j, s):
                act.wait_ge(h_ready, b * J + j + 1)
                act.activation(g[:, s, :], h[:, ds(j * TB, TB)], ACT.Abs).then_inc(h_abs_ready, 1)

            def squares(b):
                act.wait_ge(xr_loaded, (b + 1) * 16)
                if not isinstance(b, int) or b >= 1:
                    act.wait_ge(rs_ready, b)
                junk = square_junk[b if isinstance(b, int) and b <= 1 else 2]
                if not isinstance(b, int) or b >= 2:
                    act.wait_ge(dw_ready, ND - WS + 1)
                for i in range(TT // 2 if isinstance(b, int) and b == 0 else TT):
                    last = act.activation(junk[:, i * D:(i + 1) * D], xr[:, ds((b % XS) * (TT * D) + i * D, D)],
                                          ACT.Square, accum_out=sumsq[:, i:i + 1])
                last.then_inc(sumsq_ready, 1)

            def high(b, kt):
                act.wait_ge(xn_ready, b * KT + kt + 1)
                if not isinstance(b, int) or b >= 2:
                    act.wait_ge(val_ready, (b - 1) * J)
                act.copy(x_hi[:, ds((b % 2) * (KT * TB) + kt * TB, TB)], xn[:, kt % 2, :]).then_inc(x_hi_ready, 1)

            def weight_bound(j, slot):
                act.wait_ge(up_loaded[j % WS], (j // WS + 1) * 16)
                if j == 1:
                    act.wait_ge(cs_peak_all, 1)
                if j >= 2:
                    act.wait_ge(w_bound_all, j - 1)
                act.activation(bound_junk[:, slot * WJ:(slot + 1) * WJ], w_raw[:, j % WS, :], ACT.Abs,
                               accum_out=peak[:, slot:slot + 1]).then_inc(w_bound, 1)

            def weight_high(j, slot):
                act.wait_ge(w_scaled, j + 1)
                act.activation(w_hi[:, ds(j * WJ, WJ)], w_raw[:, j % WS, :], ACT.Copy,
                               scale=w_scale[:, slot:slot + 1]).then_inc(w_hi_ready, 1)

            def sum_down(chunk, slot):
                act.wait_ge(down_sum_loaded[slot], (chunk // 2 + 1) * 16)
                if not isinstance(chunk, int) or chunk >= 2:
                    act.wait_ge(d_summed, chunk - 1)
                act.activation(sum_junk[:, slot * WJ:(slot + 1) * WJ], down_sum_raw[:, slot, :], ACT.Abs,
                               accum_out=d_sums[:, ds(chunk, 1)]).then_inc(d_summed, 1)

            squares(0)
            weight_bound(0, 0)
            weight_high(0, 0)
            high(0, 0)
            high(0, 1)
            weight_bound(1, 1)
            high(0, 2)
            high(0, 3)
            weight_high(1, 1)
            weight_bound(2, 0)
            for j in range(J):
                if j + 2 < J:
                    weight_high(j + 2, j % 2)
                gelu(0, j, j % 2, first=j < 2)
                if j + 3 < J:
                    weight_bound(j + 3, (j + 1) % 2)
                absolute(0, j, j % 2)
                if j in SUM_AT:
                    sum_down(SUM_AT.index(j), SUM_AT.index(j) % 2)
                if j == RSQRT_AT - 1:
                    squares(1)
                if NORM_AT <= j < NORM_AT + KT:
                    high(1, j - NORM_AT)

            def pair(b, j, s):
                gelu(b, j, s)
                absolute(b, j, s)

            def up_block(b, last=False):
                with act.Fori(0, 2) as i:
                    for s in range(2):
                        pair(b, 2 * i + s, s)
                if not last:
                    squares(b + 1)
                with act.Fori(2, 4) as i:
                    for s in range(2):
                        pair(b, 2 * i + s, s)
                for k in range(4):
                    pair(b, 8 + k, k % 2)
                    if not last:
                        high(b + 1, k)
                with act.Fori(6, 8) as i:
                    for s in range(2):
                        pair(b, 2 * i + s, s)

            with act.Fori(1, NB - 1) as b:
                up_block(b)
            up_block(NB - 1, last=True)
            for j in range(1, J, 2):
                at = slice(j * TB, (j + 1) * TB)
                act.wait_ge(scaled_ready, (NB - 1) * J + j + 1)
                act.activation(h[:, at], h[:, at], ACT.Copy, bias=ROUND).then_inc(round_step, 1)
                act.wait_ge(round_step, (j + 1) // 2)
                act.activation(q_last[:, at], h[:, at], ACT.Copy, bias=-ROUND).then_inc(q_act_ready, 1)

        @block.gpsimd
        def _(pool):
            pool.memset(ident[:], 0.0).then_inc(ident_ready, 1)
            pool.wait_ge(ident_ready, 1)
            pool.affine_select(out=ident[:], in_=ident[:], compare_op=ALU.not_equal, fill=1.0, base=0,
                               pattern=[[-1, P]], channel_multiplier=1).then_inc(ident_ready, 1)

            def weight_bound_all(j):
                pool.wait_ge(w_bound, j + 1)
                at = slice(j % 2, j % 2 + 1)
                pool.partition_all_reduce(peak_all[:, at], peak[:, at], P, RMAX).then_inc(w_bound_all, 1)

            pool.wait_ge(cs_peak, 1)
            pool.partition_all_reduce(peak_all[:, 1:2], peak[:, 1:2], P, RMAX).then_inc(cs_peak_all, 1)
            for j in range(J):
                weight_bound_all(j)
            pool.wait_ge(d_sum_ready, 1)
            pool.partition_all_reduce(d_total[:], d_sum[:], P, RADD).then_inc(d_total_ready, 1)
            pool.wait_ge(d_scale_ready, 1)
            for i in range(ND // 2):
                for s in range(2):
                    c = 2 * i + s
                    raw = w_raw[:, c % WS, :]
                    pool.wait_ge(down_loaded[c % WS], (c // WS + 1) * 16)
                    pool.tensor_scalar(raw, raw, d_scale[:], ROUND, ALU.mult, ALU.add).then_inc(d_pass, 1)
                    pool.wait_ge(d_pass, 2 * c + 1)
                    pool.tensor_scalar(raw, raw, -ROUND, 1.0, ALU.add, ALU.mult).then_inc(d_pass, 1)
                    pool.wait_ge(d_pass, 2 * c + 2)
                    pool.tensor_scalar(dw[:, ds(c * WJ, WJ)], raw, 1.0, -1.0, ALU.min, ALU.max).then_inc(dw_ready, 1)

        @block.vector
        def _(dve):
            def power_of_two(slot, step, count, top, scale):
                a, p = peak_all[:, slot:slot + 1], p2[:, slot:slot + 1]
                dve.tensor_scalar(a, a, 2.0 ** -100, 2.0 ** 110, ALU.max, ALU.min).then_inc(step, 1)
                dve.wait_ge(step, count + 1)
                dve.tensor_scalar(p.bitcast(I32), a.bitcast(I32), EXPONENT, None, ALU.bitwise_and).then_inc(step, 1)
                dve.wait_ge(step, count + 2)
                return dve.tensor_scalar(scale.bitcast(I32), p.bitcast(I32), -1.0,
                                         float((254 << 23) + int(math.log2(top)) * (1 << 23)), ALU.mult, ALU.add)

            def weight_scale(j, slot):
                dve.wait_ge(w_bound_all, j + 1)
                power_of_two(slot, w_step, 2 * j, W_TOP, w_scale[:, slot:slot + 1]).then_inc(w_scaled, 1)
                dve.tensor_scalar(w_unscale[:, j:j + 1], p2[:, slot:slot + 1], cs_unscale[:], None,
                                  ALU.mult).then_inc(w_unscaled, 1)

            def weight_low(j, slot):
                dve.wait_ge(w_scaled, j + 1)
                dve.wait_ge(w_hi_ready, j + 1)
                at = ds(j * WJ, WJ)
                dve.scalar_tensor_tensor(out=w_lo[:, at], in0=w_raw[:, j % WS, :], scalar=w_scale[:, slot:slot + 1],
                                         in1=w_hi[:, at], op0=ALU.mult, op1=ALU.subtract).then_inc(w_ready, 1)

            def rsqrt(b):
                base = b * RS_STEPS
                dve.wait_ge(sumsq_ready, b + 1)
                if isinstance(b, int) and b == 0:
                    dve.wait_ge(sumsq_dve_ready, 1)
                if not isinstance(b, int) or b >= 1:
                    dve.wait_ge(rs_rows, b)
                dve.tensor_scalar(ms[:], sumsq[:], 1.0 / D, EPS, ALU.mult, ALU.add).then_inc(rs_step, 1)
                dve.wait_ge(rs_step, base + 1)
                dve.tensor_scalar(rs_t[:].bitcast(I32), ms[:].bitcast(I32), 1, None,
                                  ALU.logical_shift_right).then_inc(rs_step, 1)
                dve.wait_ge(rs_step, base + 2)
                dve.tensor_scalar(rs[:].bitcast(I32), rs_t[:].bitcast(I32), -1.0, float(RSQRT_SEED),
                                  ALU.mult, ALU.add).then_inc(rs_step, 1)
                dve.wait_ge(rs_step, base + 3)
                for k in range(3):
                    dve.tensor_tensor(rs_t[:], rs[:], rs[:], ALU.mult).then_inc(rs_step, 1)
                    dve.wait_ge(rs_step, base + 3 * k + 4)
                    dve.scalar_tensor_tensor(out=rs_t[:], in0=rs_t[:], scalar=-0.5, in1=ms[:],
                                             op0=ALU.mult, op1=ALU.mult).then_inc(rs_step, 1)
                    dve.wait_ge(rs_step, base + 3 * k + 5)
                    last = dve.scalar_tensor_tensor(out=rs[:], in0=rs_t[:], scalar=1.5, in1=rs[:],
                                                    op0=ALU.add, op1=ALU.mult)
                    if k < 2:
                        last.then_inc(rs_step, 1)
                        dve.wait_ge(rs_step, base + 3 * k + 6)
                    else:
                        last.then_inc(rs_ready, 1)

            def norm(b, kt):
                dve.wait_ge(rs_rows, b + 1)
                dve.wait_ge(xt_loaded, (b + 1) * 16)
                if kt >= 2:
                    dve.wait_ge(x_lo_ready, b * KT + kt - 1)
                elif not isinstance(b, int) or b >= 1:
                    dve.wait_ge(x_lo_ready, b * KT + kt - 1)
                dve.scalar_tensor_tensor(out=xn[:, kt % 2, :], in0=xt_raw[:, kt * TB:(kt + 1) * TB],
                                         scalar=cs[:, ds(kt * B + b // PER_B, 1)], in1=ps_m[:],
                                         op0=ALU.mult, op1=ALU.mult).then_inc(xn_ready, 1)

            def low(b, kt):
                at = ds((b % 2) * (KT * TB) + kt * TB, TB)
                dve.wait_ge(x_hi_ready, b * KT + kt + 1)
                dve.tensor_tensor(x_lo[:, at], xn[:, kt % 2, :], x_hi[:, at], ALU.subtract).then_inc(x_lo_ready, 1)

            def hidden(b, j, s, first=False):
                n = b * J + j
                at = ds(j * TB, TB)
                dve.wait_ge(val_ready, n + 1)
                dve.wait_ge(g_ready, n + 1)
                if not first:
                    dve.wait_ge(scaled_ready, n - J + 1)
                dve.scalar_tensor_tensor(out=h[:, at], in0=ps_u[:, 2 * s, :], scalar=w_unscale[:, ds(j, 1)],
                                         in1=g[:, s, :], op0=ALU.mult, op1=ALU.mult).then_inc(h_ready, 1)

            def peak_of(b, j, s, first=False):
                n = b * J + j
                dve.wait_ge(h_abs_ready, n + 1)
                if isinstance(j, int) and j == 0:
                    if not first:
                        dve.wait_ge(max_rows, b)
                    dve.tensor_copy(h_max[:], g[:, s, :]).then_inc(h_max_ready, 1)
                else:
                    dve.wait_ge(h_max_ready, n)
                    dve.tensor_tensor(h_max[:], g[:, s, :], h_max[:], ALU.max).then_inc(h_max_ready, 1)

            def row_scales(b, dequant=dequant):
                dve.wait_ge(max_rows, b + 1)
                dve.tensor_reduce(row_max[:], ps_m[:].rearrange("p (i n) -> p i n", i=TT), AX.X,
                                  ALU.max).then_inc(row_step, 1)
                dve.wait_ge(row_step, 3 * b + 1)
                dve.tensor_scalar(row_max[:], row_max[:], CLIP, None, ALU.max).then_inc(row_step, 1)
                dve.wait_ge(row_step, 3 * b + 2)
                dve.reciprocal(row_rec[:], row_max[:]).then_inc(row_step, 1)
                dve.wait_ge(row_step, 3 * b + 3)
                dve.tensor_scalar(row_scale[:], row_rec[:], QMAX, None, ALU.mult).then_inc(scale_ready, 1)
                dve.tensor_scalar(dequant[:], row_max[:], 1.0 / QMAX, d_mean[:], ALU.mult,
                                  ALU.mult).then_inc(dequant_ready, 1)

            def quantize(b, t):
                for s in range(2):
                    m = b * J + t + s
                    if isinstance(t, int) and t == 0:
                        dve.wait_ge(scale_rows, b + 1)
                    if not (isinstance(t, int) and t == 0):
                        dve.wait_ge(q_ready, m - 1)
                    dve.tensor_tensor(scaled[:, s, :], h[:, ds((t + s) * TB, TB)], ps_s[:],
                                      ALU.mult).then_inc(scaled_ready, 1)
                for s in range(2):
                    m = b * J + t + s
                    dve.wait_ge(scaled_ready, m + 1)
                    dve.tensor_scalar(q[:, ds((t + s) * TB, TB)], scaled[:, s, :], ROUND, ROUND, ALU.add,
                                      ALU.subtract).then_inc(q_ready, 1)

            def residual(b, i, bank, dequant=dequant):
                at = ds((b % XS) * (TT * D) + i * D, D)
                dve.wait_ge(y_ready, b * TT + i + 1)
                dve.wait_ge(dequant_ready, b + 1)
                dve.scalar_tensor_tensor(out=xr[:, at], in0=bank, scalar=dequant[:, i:i + 1], in1=xr[:, at],
                                         op0=ALU.mult, op1=ALU.add).then_inc(y_done, 1)

            dve.wait_ge(cs_matmul, 1)
            dve.tensor_scalar(cs_raw[:], ps_y[:, 0, 0:KT * B], 1.0, None, ALU.add).then_inc(cs_step, 1)
            dve.wait_ge(cs_step, 1)
            dve.tensor_reduce(peak[:, 1:2], cs_raw[:], AX.X, ALU.max, apply_absolute_value=True).then_inc(cs_peak, 1)
            dve.wait_ge(cs_peak_all, 1)
            power_of_two(1, cs_step, 1, X_TOP, cs_scale[:]).then_inc(cs_step, 1)
            dve.tensor_scalar(cs_unscale[:], p2[:, 1:2], 1.0 / (W_TOP * X_TOP), None, ALU.mult).then_inc(cs_step, 1)
            dve.wait_ge(cs_step, 4)
            dve.tensor_scalar(cs[:], cs_raw[:], cs_scale[:], None, ALU.mult).then_inc(cs_step, 1)
            dve.wait_ge(cs_step, 6)
            dve.wait_ge(xr_loaded, 16)
            for i in range(TT // 2, TT):
                x_tile = xr[:, i * D:(i + 1) * D]
                last = dve.scalar_tensor_tensor(out=square_junk[0][:, i * D:(i + 1) * D], in0=x_tile, scalar=1.0,
                                                in1=x_tile, op0=ALU.mult, op1=ALU.mult, accum_out=sumsq[:, i:i + 1])
            last.then_inc(sumsq_dve_ready, 1)
            rsqrt(0)
            weight_scale(0, 0)
            norm(0, 0)
            norm(0, 1)
            weight_low(0, 0)
            low(0, 0)
            low(0, 1)
            norm(0, 2)
            norm(0, 3)
            low(0, 2)
            weight_scale(1, 1)
            low(0, 3)
            weight_low(1, 1)
            for j in range(J):
                if j + 2 < J:
                    weight_scale(j + 2, j % 2)
                if j >= 1:
                    peak_of(0, j - 1, (j - 1) % 2, first=True)
                if j + 2 < J:
                    weight_low(j + 2, j % 2)
                hidden(0, j, j % 2, first=True)
                if j == RSQRT_AT:
                    rsqrt(1)
                if j == SUM_AT[-1] + 1:
                    dve.wait_ge(d_summed, ND)
                    dve.tensor_reduce(d_sum[:], d_sums[:], AX.X, ALU.add).then_inc(d_sum_ready, 1)
                if NORM_AT <= j < NORM_AT + KT:
                    norm(1, j - NORM_AT)
                    low(1, j - NORM_AT)
                if j == SUM_AT[-1] + 2:
                    dve.wait_ge(d_total_ready, 1)
                    dve.tensor_scalar(d_mean[:], d_total[:], 1.0 / (J * P * D), CLIP, ALU.mult,
                                      ALU.max).then_inc(d_step, 1)
                    dve.wait_ge(d_step, 1)
                    dve.reciprocal(d_scale[:], d_mean[:]).then_inc(d_scale_ready, 1)
            peak_of(0, J - 1, (J - 1) % 2, first=True)

            def up_block(b, last=False):
                row_scales(b - 1)
                quantize(b - 1, 0)
                hidden(b, 0, 0)
                quantize(b - 1, 2)
                peak_of(b, 0, 0)
                hidden(b, 1, 1)
                quantize(b - 1, 4)
                peak_of(b, 1, 1)
                with dve.Fori(1, 3) as i:
                    for s in range(2):
                        hidden(b, 2 * i + s, s)
                        quantize(b - 1, 4 * i + 2 * s + 2)
                        peak_of(b, 2 * i + s, s)
                if not last:
                    rsqrt(b + 1)
                hidden(b, 6, 0)
                quantize(b - 1, J - 2)
                peak_of(b, 6, 0)
                hidden(b, 7, 1)
                peak_of(b, 7, 1)
                for k in range(4):
                    hidden(b, 8 + k, k % 2)
                    if not last:
                        norm(b + 1, k)
                        low(b + 1, k)
                    peak_of(b, 8 + k, k % 2)
                    if not (last and k >= 2):
                        residual(b - 1, k, ps_y[:, k % 2, :])
                with dve.Fori(6, 8) as i:
                    for s in range(2):
                        hidden(b, 2 * i + s, s)
                        peak_of(b, 2 * i + s, s)

            with dve.Fori(1, NB - 1) as b:
                up_block(b)
            up_block(NB - 1, last=True)
            row_scales(NB - 1, dequant_last)
            residual(NB - 2, 2, ps_y[:, 0, :])

            for j in range(J):
                at = slice(j * TB, (j + 1) * TB)
                if j == 0:
                    dve.wait_ge(scale_rows, NB)
                dve.tensor_tensor(h[:, at], h[:, at], ps_s[:], ALU.mult).then_inc(scaled_ready, 1)
                if j % 2 == 1:
                    at = slice((j - 1) * TB, j * TB)
                    dve.wait_ge(scaled_ready, (NB - 1) * J + j)
                    dve.tensor_scalar(q_last[:, at], h[:, at], ROUND, ROUND, ALU.add,
                                      ALU.subtract).then_inc(q_ready, 1)
                if j == 3:
                    residual(NB - 2, 3, ps_y[:, 1, :])
            for i in range(TT):
                residual(NB - 1, i, ps_u[:, i, :], dequant_last)


def kernel(x, cond_256, L0_cond_norm_w, L0_cond_up_w, L0_cond_down_w):
    import numpy as _np
    import concourse.bacc as _bacc
    from concourse import mybir as _mybir
    from concourse.bass_utils import run_bass_kernel_spmd as _run

    x = _np.asarray(x)
    up, down = _np.asarray(L0_cond_up_w), _np.asarray(L0_cond_down_w)
    S0, S1, D = x.shape
    FF = down.shape[1]
    TB, KT, J = 512, D // 128, FF // 128
    rows = x.reshape(S0 * S1, D)
    laid = {
        "x_rows": rows,
        "x_cols": rows.reshape(-1, 128, TB // 128, KT, 128).transpose(0, 4, 3, 2, 1).reshape(-1, 128, KT * TB),
        "cond_t": _np.asarray(cond_256).T,
        "norm_t": _np.asarray(L0_cond_norm_w).T,
        "up_t": up.reshape(2, J, 128, KT, 128).transpose(1, 4, 0, 3, 2).reshape(J, 128, 2 * KT * 128),
        "down_t": down.reshape(D, J, 128).transpose(2, 1, 0).reshape(128, J * D),
    }
    nc = _bacc.Bacc("TRN2", target_bir_lowering=False, num_devices=1)
    arrays, args = {}, []
    for name, a in laid.items():
        a = _np.ascontiguousarray(a)
        arrays[f"in_{name}_dram"] = a
        args.append(nc.dram_tensor(f"in_{name}_dram", a.shape, _mybir.dt.from_np(a.dtype), kind="ExternalInput").ap())
    args.append(nc.dram_tensor("out_0_dram", rows.shape, _mybir.dt.float32, kind="ExternalOutput").ap())
    bass_cond_norm_geglu_bitlinear(nc, *args)
    r = _run(nc, [arrays], core_ids=[0])
    return r.results[0]["out_0_dram"].reshape(x.shape)
```
